# Optimizing a Trainium2 kernel written in Bass

```python
import numpy as np
import jax
import jax.numpy as jnp

def _softmax(x, axis=-1):
    return jax.nn.softmax(x, axis=axis)

def _gelu(x):
    return jax.nn.gelu(x, approximate=True)

def _silu(x):
    return jax.nn.silu(x)

def _sigmoid(x):
    return jax.nn.sigmoid(x)

def _layernorm(x, axis=-1, eps=1e-05):
    m = jnp.mean(x, axis=axis, keepdims=True)
    v = jnp.var(x, axis=axis, keepdims=True)
    return (x - m) / jnp.sqrt(v + eps)

def _scatter_add(tgt, idx, src, axis=0):
    return tgt.at[idx].add(src)

def _segment_sum(src, seg, n):
    return jax.ops.segment_sum(src, seg, n)
kernel_name = 'mk_cond_resid_d4_seqx_r8_704b70'

def setup_inputs(seed: int=0):
    np.random.seed(seed)
    _w = jnp.asarray

    def _rec_inputs():
        import jax
        import jax.numpy as jnp
        _rk = jax.random.key(seed)
        x = -0.000125 + 0.9999 * jax.random.normal(jax.random.fold_in(_rk, 1), (8, 128, 512), jnp.float32)
        _lenS = 128 - jax.random.randint(jax.random.fold_in(_rk, 7), (8,), 0, max(1, 128 // 4) + 1, jnp.int32)
        _lenS2 = 128 - jax.random.randint(jax.random.fold_in(_rk, 8), (8,), 0, max(1, 128 // 4) + 1, jnp.int32)
        itok_B_0_7 = jax.random.randint(jax.random.fold_in(_rk, 11), (8,), 0, 8, jnp.int32)
        itok_B_0_2 = jax.random.randint(jax.random.fold_in(_rk, 12), (8,), 0, 3, jnp.int32)
        itok_Bx16_0_63 = jax.random.randint(jax.random.fold_in(_rk, 13), (8, 16), 0, 64, jnp.int32)
        itok_B_207_1644 = jax.random.randint(jax.random.fold_in(_rk, 14), (8,), 207, 1645, jnp.int32)
        itok_B_0_23 = jax.random.randint(jax.random.fold_in(_rk, 15), (8,), 0, 24, jnp.int32)
        return (x, itok_B_0_7, itok_B_0_2, itok_Bx16_0_63, itok_B_207_1644, itok_B_0_23)
    x, itok_B_0_7, itok_B_0_2, itok_Bx16_0_63, itok_B_207_1644, itok_B_0_23 = _rec_inputs()

    def _L0_cond_setup():
        import jax, jax.numpy as jnp
        import numpy as np
        TOP_K = 2
        LANG_BIAS = 5.0
        SCALING = 32.0 / 16.0
        LANGUAGE_PAD_ID = -1
        key = jax.random.key(seed)
        ks = jax.random.split(key, 6)
        B, T, D, O, E, R = (4, 256, 512, 512, 8, 16)
        x = jax.random.normal(ks[0], (B, T, D), dtype=jnp.float32)
        language_ids = jax.random.randint(ks[1], (B,), 0, E).astype(jnp.int64)
        W = jax.random.normal(ks[2], (O, D), dtype=jnp.float32) * (1.0 / np.sqrt(D))
        Wr = jax.random.normal(ks[3], (E, D), dtype=jnp.float32) * (1.0 / np.sqrt(D))
        A = jax.random.normal(ks[4], (E, R, D), dtype=jnp.float32) * (1.0 / np.sqrt(D))
        Bm = jax.random.normal(ks[5], (O, R), dtype=jnp.float32) * 0.0
        Bm = jnp.broadcast_to(Bm, (E, O, R)) + jax.random.normal(ks[5], (E, O, R), dtype=jnp.float32) * 0.02
        return {'x': x, 'language_ids': language_ids, 'W': W, 'Wr': Wr, 'A': A, 'B': Bm}
    _L0_cond_all = _L0_cond_setup()
    _L0_cond_in = {k: v for k, v in _L0_cond_all.items() if k in ('W', 'Wr', 'A', 'B')}
    del _L0_cond_all

    def _L1_cond_setup():
        import jax, jax.numpy as jnp
        import numpy as np
        B, S, D_IN, D_OUT = (4, 256, 512, 512)
        R, NUM_LABELERS = (32, 5)
        LORA_SCALING = 16 / 32
        key = jax.random.key(seed)
        k1, k2, k3, k4, k5 = jax.random.split(key, 5)
        x = jax.random.normal(k1, (B, S, D_IN), dtype=jnp.float32)
        labeler_index = jax.random.randint(k2, (B,), 0, NUM_LABELERS, dtype=jnp.int64)
        W = jax.random.normal(k3, (D_OUT, D_IN), dtype=jnp.float32) * 0.02
        lora_A = jax.random.normal(k4, (NUM_LABELERS, D_IN, R), dtype=jnp.float32) * 0.02
        lora_B_w = jax.random.normal(k5, (D_OUT, R), dtype=jnp.float32) * 0.02
        return {'x': x, 'labeler_index': labeler_index, 'W': W, 'lora_A': lora_A, 'lora_B_w': lora_B_w}
    _L1_cond_all = _L1_cond_setup()
    _L1_cond_in = {k: v for k, v in _L1_cond_all.items() if k in ('W', 'lora_A', 'lora_B_w')}
    del _L1_cond_all

    def _L2_cond_setup():
        import jax, jax.numpy as jnp
        import numpy as np
        B, S, HID = (4, 128, 512)
        D, HQ, HK = (128, 32, 8)
        PAGES, PSIZE, NPP = (64, 32, 16)
        THETA = 10000.0
        EPS = 1e-06
        SCALE = 1.0 / float(np.sqrt(D))

        def _rmsnorm(t, w):
            var = jnp.mean(t * t, axis=-1, keepdims=True)
            return t * jax.lax.rsqrt(var + EPS) * w

        def _rope(t, pos):
            inv_freq = 1.0 / THETA ** (jnp.arange(0, D, 2, dtype=jnp.float32) / D)
            freqs = pos[..., None].astype(jnp.float32) * inv_freq
            cos = jnp.cos(freqs)[:, :, None, :]
            sin = jnp.sin(freqs)[:, :, None, :]
            t1, t2 = (t[..., :D // 2], t[..., D // 2:])
            return jnp.concatenate([t1 * cos - t2 * sin, t2 * cos + t1 * sin], axis=-1)
        key = jax.random.key(seed)
        ks = jax.random.split(key, 10)
        x = jax.random.normal(ks[0], (B, S, HID), jnp.float32)
        Wq = jax.random.normal(ks[1], (HQ * D, HID), jnp.float32) * 0.02
        Wk = jax.random.normal(ks[2], (HK * D, HID), jnp.float32) * 0.02
        Wv = jax.random.normal(ks[3], (HK * D, HID), jnp.float32) * 0.02
        Wo = jax.random.normal(ks[4], (HID, HQ * D), jnp.float32) * 0.02
        q_norm_w = jax.random.uniform(ks[5], (D,), jnp.float32)
        k_norm_w = jax.random.uniform(ks[6], (D,), jnp.float32)
        k_cache = jax.random.normal(ks[7], (PAGES, PSIZE, HK, D), jnp.float32)
        v_cache = jax.random.normal(ks[8], (PAGES, PSIZE, HK, D), jnp.float32)
        block_table = jnp.arange(B * NPP, dtype=jnp.int32).reshape(B, NPP)
        cache_seqlens = jax.random.randint(ks[9], (B,), 0, 475).astype(jnp.int32)
        return dict(x=x, Wq=Wq, Wk=Wk, Wv=Wv, Wo=Wo, q_norm_w=q_norm_w, k_norm_w=k_norm_w, k_cache=k_cache, v_cache=v_cache, block_table=block_table, cache_seqlens=cache_seqlens)
    _L2_cond_all = _L2_cond_setup()
    _L2_cond_in = {k: v for k, v in _L2_cond_all.items() if k in ('Wq', 'Wk', 'Wv', 'Wo', 'q_norm_w', 'k_norm_w', 'k_cache', 'v_cache')}
    del _L2_cond_all

    def _L3_cond_setup():
        import jax, jax.numpy as jnp
        import numpy as np
        R = 16
        ALPHA = 32
        SCALING = ALPHA / R
        SLOTS = 32
        IN_F = 512
        OUT_F = 512
        B, T = (8, 128)
        key = jax.random.key(seed)
        k1, k2, k3, k4, k5, k6 = jax.random.split(key, 6)
        x = jax.random.normal(k1, (B, T, IN_F), dtype=jnp.float32)
        adapter_mapping = jax.random.randint(k2, (B,), 0, SLOTS, dtype=jnp.int32)
        W = jax.random.normal(k3, (OUT_F, IN_F), dtype=jnp.float32) * 0.02
        b = jax.random.normal(k4, (OUT_F,), dtype=jnp.float32) * 0.02
        lora_As = jax.random.normal(k5, (SLOTS, IN_F, R), dtype=jnp.float32) * 0.02
        lora_Bs = jax.random.normal(k6, (SLOTS, R, OUT_F), dtype=jnp.float32) * 0.02
        return {'x': x, 'adapter_mapping': adapter_mapping, 'W': W, 'b': b, 'lora_As': lora_As, 'lora_Bs': lora_Bs}
    _L3_cond_all = _L3_cond_setup()
    _L3_cond_in = {k: v for k, v in _L3_cond_all.items() if k in ('W', 'b', 'lora_As', 'lora_Bs')}
    del _L3_cond_all
    return {'x': x, 'itok_B_0_7': itok_B_0_7, 'itok_B_0_2': itok_B_0_2, 'itok_Bx16_0_63': itok_Bx16_0_63, 'itok_B_207_1644': itok_B_207_1644, 'itok_B_0_23': itok_B_0_23, 'L0_cond_W': _L0_cond_in['W'], 'L0_cond_Wr': _L0_cond_in['Wr'], 'L0_cond_A': _L0_cond_in['A'], 'L0_cond_B': _L0_cond_in['B'], 'L1_cond_W': _L1_cond_in['W'], 'L1_cond_lora_A': _L1_cond_in['lora_A'], 'L1_cond_lora_B_w': _L1_cond_in['lora_B_w'], 'L2_cond_Wq': _L2_cond_in['Wq'], 'L2_cond_Wk': _L2_cond_in['Wk'], 'L2_cond_Wv': _L2_cond_in['Wv'], 'L2_cond_Wo': _L2_cond_in['Wo'], 'L2_cond_q_norm_w': _L2_cond_in['q_norm_w'], 'L2_cond_k_norm_w': _L2_cond_in['k_norm_w'], 'L2_cond_k_cache': _L2_cond_in['k_cache'], 'L2_cond_v_cache': _L2_cond_in['v_cache'], 'L3_cond_W': _L3_cond_in['W'], 'L3_cond_b': _L3_cond_in['b'], 'L3_cond_lora_As': _L3_cond_in['lora_As'], 'L3_cond_lora_Bs': _L3_cond_in['lora_Bs']}

def reference(x, itok_B_0_7, itok_B_0_2, itok_Bx16_0_63, itok_B_207_1644, itok_B_0_23, L0_cond_W, L0_cond_Wr, L0_cond_A, L0_cond_B, L1_cond_W, L1_cond_lora_A, L1_cond_lora_B_w, L2_cond_Wq, L2_cond_Wk, L2_cond_Wv, L2_cond_Wo, L2_cond_q_norm_w, L2_cond_k_norm_w, L2_cond_k_cache, L2_cond_v_cache, L3_cond_W, L3_cond_b, L3_cond_lora_As, L3_cond_lora_Bs):
    import jax
    import jax.numpy as jnp

    def _L0_cond_ref(x, language_ids, W, Wr, A, B):
        import jax, jax.numpy as jnp
        import numpy as np
        TOP_K = 2
        LANG_BIAS = 5.0
        SCALING = 32.0 / 16.0
        LANGUAGE_PAD_ID = -1
        base = jnp.einsum('btd,od->bto', x, W)
        E = Wr.shape[0]
        logits = jnp.einsum('btd,ed->bte', x.astype(jnp.float32), Wr.astype(jnp.float32))
        expert_targets = language_ids
        valid = expert_targets >= 0
        tgt = jnp.where(valid, expert_targets, 0)
        bias = jax.nn.one_hot(tgt, E, dtype=logits.dtype) * LANG_BIAS
        bias = jnp.where(valid[:, None], bias, 0.0)
        logits = logits + bias[:, None, :]
        topw, topi = jax.lax.top_k(logits, TOP_K)
        weights = jax.nn.softmax(topw, axis=-1)
        gates = jnp.sum(jax.nn.one_hot(topi, E, dtype=weights.dtype) * weights[..., None], axis=-2)
        gates = gates.astype(x.dtype)
        h = jnp.einsum('btd,erd->bter', x, A)
        lora_out = jnp.einsum('bter,bte,eor->bto', h, gates, B)
        return base + SCALING * lora_out

    def _L1_cond_ref(x, labeler_index, W, lora_A, lora_B_w):
        import jax, jax.numpy as jnp
        import numpy as np
        B, S, D_IN, D_OUT = (4, 256, 512, 512)
        R, NUM_LABELERS = (32, 5)
        LORA_SCALING = 16 / 32
        base = jnp.einsum('bsi,oi->bso', x, W)
        labelers_A = lora_A[labeler_index]
        low = jnp.einsum('bsi,bir->bsr', x, labelers_A)
        delta = jnp.einsum('bsr,or->bso', low, lora_B_w) * LORA_SCALING
        return base + delta

    def _L2_cond_ref(x, Wq, Wk, Wv, Wo, q_norm_w, k_norm_w, k_cache, v_cache, block_table, cache_seqlens):
        import jax, jax.numpy as jnp
        import numpy as np
        B, S, HID = (4, 128, 512)
        D, HQ, HK = (128, 32, 8)
        PAGES, PSIZE, NPP = (64, 32, 16)
        THETA = 10000.0
        EPS = 1e-06
        SCALE = 1.0 / float(np.sqrt(D))

        def _rmsnorm(t, w):
            var = jnp.mean(t * t, axis=-1, keepdims=True)
            return t * jax.lax.rsqrt(var + EPS) * w

        def _rope(t, pos):
            inv_freq = 1.0 / THETA ** (jnp.arange(0, D, 2, dtype=jnp.float32) / D)
            freqs = pos[..., None].astype(jnp.float32) * inv_freq
            cos = jnp.cos(freqs)[:, :, None, :]
            sin = jnp.sin(freqs)[:, :, None, :]
            t1, t2 = (t[..., :D // 2], t[..., D // 2:])
            return jnp.concatenate([t1 * cos - t2 * sin, t2 * cos + t1 * sin], axis=-1)
        bsz, seqlen, _ = x.shape
        q = jnp.einsum('bsd,ed->bse', x, Wq).reshape(bsz, seqlen, HQ, D)
        k = jnp.einsum('bsd,ed->bse', x, Wk).reshape(bsz, seqlen, HK, D)
        v = jnp.einsum('bsd,ed->bse', x, Wv).reshape(bsz, seqlen, HK, D)
        q = _rmsnorm(q, q_norm_w)
        k = _rmsnorm(k, k_norm_w)
        pos = cache_seqlens[:, None] + jnp.arange(seqlen)[None, :]
        q = _rope(q, pos)
        k = _rope(k, pos)
        L = NPP * PSIZE
        kc = k_cache[block_table].reshape(bsz, L, HK, D)
        vc = v_cache[block_table].reshape(bsz, L, HK, D)
        k_all = jnp.concatenate([kc, k], axis=1)
        v_all = jnp.concatenate([vc, v], axis=1)
        valid_c = jnp.arange(L)[None, :] < cache_seqlens[:, None]
        valid = jnp.concatenate([valid_c, jnp.ones((bsz, seqlen), dtype=bool)], axis=1)
        rep = HQ // HK
        k_all = jnp.repeat(k_all, rep, axis=2)
        v_all = jnp.repeat(v_all, rep, axis=2)
        scores = jnp.einsum('bqhd,bkhd->bhqk', q, k_all) * SCALE
        scores = jnp.where(valid[:, None, None, :], scores, -1e+30)
        probs = jax.nn.softmax(scores, axis=-1)
        o = jnp.einsum('bhqk,bkhd->bqhd', probs, v_all)
        o = o.reshape(bsz, seqlen, HQ * D)
        return jnp.einsum('bse,de->bsd', o, Wo)

    def _L3_cond_ref(x, adapter_mapping, W, b, lora_As, lora_Bs):
        import jax, jax.numpy as jnp
        import numpy as np
        R = 16
        ALPHA = 32
        SCALING = ALPHA / R
        SLOTS = 32
        IN_F = 512
        OUT_F = 512
        B, T = (8, 128)
        base_out = jnp.einsum('bti,oi->bto', x, W) + b
        A = lora_As[adapter_mapping]
        Bm = lora_Bs[adapter_mapping]
        lora_h = jnp.einsum('bti,bir->btr', x, A)
        lora_out = jnp.einsum('btr,bro->bto', lora_h, Bm)
        return base_out + lora_out * SCALING
    x = x + _L0_cond_ref(x, itok_B_0_7, L0_cond_W, L0_cond_Wr, L0_cond_A, L0_cond_B)
    x = x + _L1_cond_ref(x, itok_B_0_2, L1_cond_W, L1_cond_lora_A, L1_cond_lora_B_w)
    x = x + _L2_cond_ref(x, L2_cond_Wq, L2_cond_Wk, L2_cond_Wv, L2_cond_Wo, L2_cond_q_norm_w, L2_cond_k_norm_w, L2_cond_k_cache, L2_cond_v_cache, itok_Bx16_0_63, itok_B_207_1644)
    x = x + _L3_cond_ref(x, itok_B_0_23, L3_cond_W, L3_cond_b, L3_cond_lora_As, L3_cond_lora_Bs)
    return x

_drawn_inputs = setup_inputs


def setup_inputs(seed=0):
    import zlib

    import numpy as np

    out = dict(_drawn_inputs(seed))
    spreads = {}
    factors = {'L0_cond_Wr': 6.736,
     'L1_cond_lora_A': 3.446,
     'L1_cond_lora_B_w': 3.413,
     'L2_cond_Wq': 3.679,
     'L2_cond_Wk': 8.0,
     'L2_cond_Wv': 6.345,
     'L2_cond_q_norm_w': 6.372,
     'L2_cond_k_norm_w': 8.0,
     'L2_cond_k_cache': 3.776,
     'L3_cond_b': 7.339}
    for name, (base, spread) in spreads.items():
        noise = np.random.default_rng([zlib.crc32(name.encode()), seed]).standard_normal(out[name].shape)
        drawn = base * np.exp(spread * noise) if base else spread * noise
        out[name] = jnp.asarray(drawn.astype(out[name].dtype))
    for name, factor in factors.items():
        out[name] = (out[name] * factor).astype(out[name].dtype)
    return out
```

```python
from contextlib import ExitStack

import numpy as np

import concourse.bass as bass
from concourse import mybir

FP32 = mybir.dt.float32
FP32R = mybir.dt.float32r
BF16 = mybir.dt.bfloat16
I32 = mybir.dt.int32
U32 = mybir.dt.uint32
ALU = mybir.AluOpType
ACT = mybir.ActivationFunctionType

B, T, DM = 8, 128, 512
P = 128
KC = DM // P
E, R0 = 8, 16
R1, R3 = 32, 16
HQ, HK, D = 32, 8, 128
REP = HQ // HK
PAGES, PSIZE, NPP = 64, 32, 16
L = NPP * PSIZE
NK = L + T
KT = NK // P
N_IT = HK * B
EPS = 1e-6
LANG_BIAS, SCALING0, SCALING1, SCALING3 = 5.0, 2.0, 0.5, 2.0
MASKED = -1e30

WG = 5120
NPIECE = 8
WPIECE = WG // NPIECE
W_Q, W_KV, W_O = 0, KC * REP * D, KC * (REP * D + 2 * D)
W_BASE0, W_AR, W_BASE1, W_BASE3 = 0, KC * DM, W_O, W_O
AR = E * R0 + E

TWO_PI = 2 * np.pi
C1 = 6.28125
C2 = float(np.float32(int((TWO_PI - C1) * 2.0**21) / 2.0**21))
C3 = float(np.float32(TWO_PI - C1 - C2))
ROUND = float(1.5 * 2**23)
PI_BELOW = float(np.float32(3.1415925))


def ge(eng, sem, value):
    if isinstance(value, int) and value <= 0:
        return
    eng.wait_ge(sem, value)


def wait_apart(eng, sem, value, passed):
    eng.wait_ge(sem, value)
    if not isinstance(value, int):
        eng.sem_inc(passed, 1)


def matmul3(pe, out, lhs, rhs, start, stop):
    pe.matmul(out, lhs[0], rhs[0], start=start, stop=False)
    pe.matmul(out, lhs[0], rhs[1], start=False, stop=False)
    return pe.matmul(out, lhs[1], rhs[0], start=False, stop=stop)


def f32(ap):
    return ap.bitcast(FP32)


def build(nc, x, xT, W, a1, b1, a3, b3, bcat0, bias3, kc, vc, q_w, k_w, inv_freq, ids, out):
    ctx = ExitStack()
    with ctx:
        def sb(name, shape, dt=FP32):
            return ctx.enter_context(nc.sbuf_tensor(name, shape, dt))

        def sem(name):
            return ctx.enter_context(nc.semaphore(name))

        resid = sb("resid", [P, B, DM])
        xTr = sb("xTr", [P, B, KC, T])
        WH = sb("WH", [P, 2 * WG], FP32R)
        WL = sb("WL", [P, 2 * WG], FP32R)
        Wraw = sb("Wraw", [P, WPIECE])
        ident = sb("ident", [P, P])
        tabs = sb("tabs", [P, B, 4, D])
        mask_all = sb("mask_all", [P, B, L], BF16)
        mask = sb("mask", [P, NK], BF16)
        idrow = sb("idrow", [1, 2 * B + B * NPP], I32)
        biasb = sb("biasb", [P, DM])
        neg_half = sb("neg_half", [P, 8])
        XH = sb("XH", [P, KC, T], FP32R)
        XL = sb("XL", [P, KC, T], FP32R)
        Kraw = sb("Kraw", [P, L // P, D])
        Vraw = sb("Vraw", [P, KT, D])
        VH = sb("VH", [P, KT, D], FP32R)
        VL = sb("VL", [P, KT, D], FP32R)
        KTH = sb("KTH", [P, NK], FP32R)
        KTL = sb("KTL", [P, NK], FP32R)
        QTH = sb("QTH", [P, REP * T], FP32R)
        QTL = sb("QTL", [P, REP * T], FP32R)
        rt1 = sb("rt1", [P, (REP + 1) * D])
        rt2 = sb("rt2", [P, (REP + 1) * D])
        roped = sb("roped", [P, (REP + 1) * D])
        knew = sb("knew", [P, D])
        S = sb("S", [P, REP, NK])
        PH = sb("PH", [P, 2, REP * T], FP32R)
        PL = sb("PL", [P, 2, REP * T], FP32R)
        OH = sb("OH", [P, REP * T], FP32R)
        OL = sb("OL", [P, REP * T], FP32R)
        squares = sb("squares", [P, (REP + 1) * D], BF16)
        ssq = sb("ssq", [P, REP + 1])
        var = sb("var", [P, REP + 1])
        rstd = sb("rstd", [P, REP + 1])
        mx = sb("mx", [P, REP])
        nbias = sb("nbias", [P, REP])
        rsum = sb("rsum", [P, REP])
        rinv = sb("rinv", [P, REP])

        SP = [ctx.enter_context(nc.psum_tensor(f"SP{i}", [P, 1024], FP32)) for i in range(2)]
        PP = [ctx.enter_context(nc.psum_tensor(f"PP{i}", [P, 512], FP32)) for i in range(2)]
        MA = ctx.enter_context(nc.psum_tensor("MA", [P, 512], FP32))
        MB = ctx.enter_context(nc.psum_tensor("MB", [P, 512], FP32))

        def wcol(piece):
            return ((piece + NPIECE) % (2 * NPIECE)) * WPIECE

        passed = sem("passed")

        def split(eng, hi, lo, src, hi_done, count):
            eng.tensor_copy(hi, src).then_inc(hi_done, 1)
            wait_apart(eng, hi_done, count, passed)
            return eng.tensor_tensor(lo, src, f32(hi), ALU.subtract)

        setup(nc, sem, locals())
        layer0(nc, sem, locals())
        lora_layer(nc, sem, locals(), "l1", a1, R1, lambda b: b1, 0, SCALING1, (W_BASE1 + WG), None)
        attention(nc, sem, locals())
        lora_layer(nc, sem, locals(), "l3", a3, R3, lambda b: b3[b, :, :], B, SCALING3, W_BASE3, out)


def setup(nc, sem, v):
    ident, tabs, mask_all, mask, neg_half, WH, WL, Wraw = (
        v[k] for k in ("ident", "tabs", "mask_all", "mask", "neg_half", "WH", "WL", "Wraw"))
    ang, turns, red = (v["S"][:, i, 0:B * D // 2].rearrange("p (b f) -> p b f", b=B) for i in range(3))
    cosv = v["S"][:, 3, 0:B * D // 2].rearrange("p (b f) -> p b f", b=B)
    sinv = v["rt2"][:, 0:B * D // 2].rearrange("p (b f) -> p b f", b=B)
    redc = v["roped"][:, 0:B * D // 2].rearrange("p (b f) -> p b f", b=B)
    keyno = v["rt1"][:, 0:L]
    invf = v["knew"][:, 0:D // 2]
    qw, kw = v["rt1"][:, 512:640], v["Kraw"][:, 0, :]
    seqi = v["Kraw"][:, 1, 0:B].bitcast(I32)
    seqf, pos, tokno = (v["Kraw"][:, 2, 16 * i:16 * i + B] for i in range(3))
    loaded, w_loaded, const, w_high, w_low, step, sin_done, cos_done, tok_in = (
        sem(f"setup_{n}") for n in ("loaded", "w_loaded", "const", "w_high", "w_low", "step", "sin", "cos", "tok"))
    ids = v["ids"]
    n_ids = 2 * B + B * NPP
    with nc.Block() as block:
        @block.sync
        def _(sp):
            for i in range(NPIECE):
                if i:
                    sp.wait_ge(w_low, i)
                sp.dma_start(Wraw[:, :], v["W"][0, :, i * WPIECE:(i + 1) * WPIECE]).then_inc(w_loaded, 16)
            sp.wait_ge(w_loaded, 16 * NPIECE)

        @block.scalar
        def _(act):
            for dst, src in (
                (seqi, ids[n_ids:n_ids + B].partition_broadcast(P)),
                (invf, v["inv_freq"].partition_broadcast(P)),
                (qw, v["q_w"].partition_broadcast(P)),
                (kw, v["k_w"].partition_broadcast(P)),
                (v["xTr"][:, :, :, :], v["xT"]),
                (v["resid"][:, :, :], v["x"].rearrange("b t d -> t b d")),
                (v["biasb"][:, :], v["bias3"].partition_broadcast(P)),
                (v["idrow"][:, :], ids[0:n_ids].rearrange("(a n) -> a n", a=1)),
            ):
                act.dma_start(dst, src).then_inc(loaded, 16)
            act.wait_ge(step, 8)
            act.activation(sinv, red, ACT.Sin).then_inc(sin_done, 1)
            act.wait_ge(step, 12)
            act.activation(cosv, redc, ACT.Sin).then_inc(cos_done, 1)
            act.wait_ge(loaded, 16 * 8)

        @block.gpsimd
        def _(pool):
            pool.iota(keyno, pattern=[[1, L]], base=0, channel_multiplier=0,
                      allow_small_or_imprecise_dtypes=True).then_inc(const, 1)
            pool.iota(tokno[:, 0:1], pattern=[[0, 1]], base=0, channel_multiplier=1,
                      allow_small_or_imprecise_dtypes=True).then_inc(const, 1)
            pool.memset(ident[:, :], 0.0).then_inc(tok_in, 1)
            wait_apart(pool, tok_in, 1, v["passed"])
            pool.affine_select(out=ident[:, :], in_=ident[:, :], compare_op=ALU.not_equal, fill=1.0, base=0,
                               pattern=[[-1, P]], channel_multiplier=1)
            pool.memset(neg_half[:, :], -0.5)
            pool.memset(mask[:, :], 0.0)
            for i in range(NPIECE):
                wait_apart(pool, w_loaded, 16 * (i + 1), v["passed"])
                c = v["wcol"](i)
                v["split"](pool, WH[:, c:c + WPIECE], WL[:, c:c + WPIECE], Wraw[:, :], w_high, i + 1).then_inc(w_low, 1)

        @block.vector
        def _(dve):
            count = [0]

            def done(ins):
                count[0] += 1
                ins.then_inc(step, 1)
                dve.wait_ge(step, count[0])

            half = [P, B, D // 2]
            dve.wait_ge(loaded, 16 * 8)
            dve.wait_ge(const, 2)
            done(dve.tensor_copy(seqf, seqi))
            done(dve.tensor_scalar(pos, seqf, tokno[:, 0:1], None, ALU.add))
            done(dve.tensor_tensor(ang, pos.unsqueeze(2).broadcast_to(half), invf.unsqueeze(1).broadcast_to(half),
                                   ALU.mult))
            done(dve.tensor_scalar(turns, ang, float(1 / TWO_PI), ROUND, ALU.mult, ALU.add))
            done(dve.tensor_scalar(turns, turns, ROUND, None, ALU.subtract))
            done(dve.scalar_tensor_tensor(out=red, in0=turns, scalar=-C1, in1=ang, op0=ALU.mult, op1=ALU.add))
            done(dve.scalar_tensor_tensor(out=ang, in0=turns, scalar=-C2, in1=red, op0=ALU.mult, op1=ALU.add))
            done(dve.scalar_tensor_tensor(out=red, in0=turns, scalar=-C3, in1=ang, op0=ALU.mult, op1=ALU.add))
            done(dve.tensor_scalar(redc, red, float(np.pi / 2), None, ALU.add))
            done(dve.tensor_scalar(turns, redc, PI_BELOW, -TWO_PI, ALU.is_gt, ALU.mult))
            done(dve.tensor_tensor(redc, redc, turns, ALU.add))
            done(dve.tensor_scalar(redc, redc, PI_BELOW, -PI_BELOW, ALU.min, ALU.max))
            dve.wait_ge(sin_done, 1)
            dve.wait_ge(cos_done, 1)
            full = [P, B, 2, D // 2]
            for n, (trig, w) in enumerate(((cosv, qw), (sinv, qw), (cosv, kw), (sinv, kw))):
                dve.tensor_tensor(tabs[:, :, n, :].rearrange("p b (a f) -> p b a f", a=2),
                                  trig.unsqueeze(2).broadcast_to(full),
                                  w.rearrange("p (a f) -> p a f", a=2).unsqueeze(1).broadcast_to(full), ALU.mult)
            for b in range(B):
                dve.tensor_scalar(mask_all[:, b, :], keyno, seqf[:, b:b + 1], MASKED, ALU.is_ge, ALU.mult)


def layer0(nc, sem, v):
    resid, xTr, XH, XL, WH, WL, Wraw, ident = (v[k] for k in ("resid", "xTr", "XH", "XL", "WH", "WL", "Wraw", "ident"))
    SP, PP, MA, MB = v["SP"], v["PP"], v["MA"], v["MB"]
    NH = E * R0
    h_all = v["S"][:, :, :].rearrange("p a b -> p (a b)")[:, 0:B * NH].rearrange("p (b n) -> p b n", b=B)
    logits = v["rt1"][:, 0:B * E].rearrange("p (b e) -> p b e", b=B)
    small = v["rt2"]
    onehot, gates, g2, top, idf, enum = (
        small[:, 64 * i:64 * i + B * E].rearrange("p (b e) -> p b e", b=B) for i in range(6))
    topi = v["roped"][:, 0:B * E].bitcast(U32).rearrange("p (b e) -> p b e", b=B)
    lang_i = v["roped"][:, 64:64 + B].bitcast(I32)
    lang, diff, ediff, esum, w0, w1 = (v["roped"][:, 128 + 16 * i:128 + 16 * i + B] for i in range(6))
    hg = v["knew"]
    BH, BL = v["PH"][:, 0, :], v["PL"][:, 0, :]
    Braw = v["Kraw"][:, :, :].rearrange("p a b -> p (a b)")
    HH, HL = v["OH"][:, 0:NH], v["OL"][:, 0:NH]
    names = ("x_high", "x_split", "w_loaded", "w_high", "w_low", "base_done", "read", "loaded", "b_high", "b_split",
             "enum", "step", "exp", "gated", "hT", "hT_high", "hT_split", "lora_done", "added")
    (x_high, x_split, w_loaded, w_high, w_low, base_done, read, loaded, b_high, b_split,
     enum_done, step, exp_done, gated, hT_done, hT_high, hT_split, lora_done, added) = (sem(f"l0_{n}") for n in names)
    n_ids = 2 * B + B * NPP
    w = WG
    with nc.Block() as block:
        @block.sync
        def _(sp):
            sp.dma_start(lang_i, v["ids"][n_ids + B:n_ids + 2 * B].partition_broadcast(P)).then_inc(loaded, 16)
            sp.dma_start(Braw, v["bcat0"]).then_inc(loaded, 16)
            for i in range(NPIECE):
                if i:
                    sp.wait_ge(w_low, i)
                sp.dma_start(Wraw[:, :], v["W"][1, :, i * WPIECE:(i + 1) * WPIECE]).then_inc(w_loaded, 16)
            sp.wait_ge(loaded, 32)

        @block.gpsimd
        def _(pool):
            pool.iota(enum, pattern=[[0, B], [1, E]], base=0, channel_multiplier=0,
                      allow_small_or_imprecise_dtypes=True).then_inc(enum_done, 1)
            wait_apart(pool, loaded, 32, v["passed"])
            v["split"](pool, BH, BL, Braw, b_high, 1).then_inc(b_split, 1)
            with pool.Fori(0, B) as b:
                wait_apart(pool, base_done, b, v["passed"])
                v["split"](pool, XH[:, :, :], XL[:, :, :], xTr[:, bass.ds(b, 1), :, :], x_high, b + 1)\
                    .then_inc(x_split, 1)
                wait_apart(pool, w_loaded, 16 * b + 16, v["passed"])
                v["split"](pool, WH[:, bass.ds(b * WPIECE, WPIECE)], WL[:, bass.ds(b * WPIECE, WPIECE)], Wraw[:, :],
                           w_high, b + 1).then_inc(w_low, 1)

        @block.tensor
        def _(pe):
            with pe.Fori(0, B) as b:
                pe.wait_ge(x_split, b + 1)
                pe.wait_ge(read, 2 * b)
                for c in range(KC):
                    base = w + W_BASE0 + c * DM
                    matmul3(pe, SP[0][:, 0:DM], (XH[:, c, :], XL[:, c, :]), (WH[:, base:base + DM], WL[:, base:base + DM]),
                            c == 0, c == KC - 1)
                for c in range(KC):
                    ar = w + W_AR + c * AR
                    last = matmul3(pe, SP[1][:, 0:AR], (XH[:, c, :], XL[:, c, :]), (WH[:, ar:ar + AR], WL[:, ar:ar + AR]),
                                   c == 0, c == KC - 1)
                last.then_inc(base_done, 1)
            pe.wait_ge(b_split, 1)
            with pe.Fori(0, B) as b:
                pe.wait_ge(gated, b + 1)
                pe.transpose(PP[0][:, 0:P], hg[:, :], ident[:, :]).then_inc(hT_done, 1)
                pe.wait_ge(hT_split, b + 1)
                pe.wait_ge(added, b)
                matmul3(pe, SP[0][:, 0:DM], (HH, HL), (BH, BL), True, True).then_inc(lora_done, 1)

        @block.scalar
        def _(act):
            act.wait_ge(step, 5)
            act.activation(ediff, diff, ACT.Exp).then_inc(exp_done, 1)
            with act.Fori(0, B) as b:
                act.wait_ge(hT_done, b + 1)
                act.activation(HH, PP[0][:, 0:P], ACT.Copy).then_inc(hT_high, 1)

        @block.vector
        def _(dve):
            with dve.Fori(0, B) as b:
                dve.wait_ge(base_done, b + 1)
                row = resid[:, bass.ds(b, 1), :].rearrange("p a d -> p (a d)")
                dve.tensor_tensor(row, SP[0][:, 0:DM], row, ALU.add).then_inc(read, 1)
                hl = h_all[:, bass.ds(b, 1), :].rearrange("p a d -> p (a d)")
                dve.tensor_copy(hl, SP[1][:, 0:NH])
                dve.tensor_copy(logits[:, bass.ds(b, 1), :].rearrange("p a d -> p (a d)"), SP[1][:, NH:AR])\
                    .then_inc(read, 1)
            dve.wait_ge(read, 2 * B)
            dve.wait_ge(loaded, 32)
            dve.wait_ge(enum_done, 1)
            count = [0]

            def done(ins):
                count[0] += 1
                ins.then_inc(step, 1)
                dve.wait_ge(step, count[0])

            all8 = [P, B, E]
            done(dve.tensor_copy(lang, lang_i))
            done(dve.tensor_tensor(onehot, enum, lang.unsqueeze(2).broadcast_to(all8), ALU.is_equal))
            done(dve.scalar_tensor_tensor(out=logits, in0=onehot, scalar=LANG_BIAS, in1=logits, op0=ALU.mult,
                                          op1=ALU.add))
            for b in range(B):
                ins = dve.max(top[:, b, :], logits[:, b, :])
            done(ins)
            done(dve.tensor_tensor(diff, top[:, :, 1], top[:, :, 0], ALU.subtract))
            for b in range(B):
                ins = dve.max_index(topi[:, b, :], top[:, b, :], logits[:, b, :])
            done(ins)
            dve.tensor_copy(idf, topi)
            dve.wait_ge(exp_done, 1)
            done(dve.tensor_scalar(esum, ediff, 1.0, None, ALU.add))
            done(dve.reciprocal(w0, esum))
            done(dve.tensor_tensor(w1, w0, ediff, ALU.mult))
            dve.tensor_tensor(gates, enum, idf[:, :, 0:1].broadcast_to(all8), ALU.is_equal)
            done(dve.tensor_tensor(g2, enum, idf[:, :, 1:2].broadcast_to(all8), ALU.is_equal))
            done(dve.tensor_tensor(gates, gates, w0.unsqueeze(2).broadcast_to(all8), ALU.mult))
            done(dve.tensor_tensor(g2, g2, w1.unsqueeze(2).broadcast_to(all8), ALU.mult))
            done(dve.tensor_tensor(gates, gates, g2, ALU.add))
            done(dve.tensor_scalar(gates, gates, SCALING0, None, ALU.mult))
            with dve.Fori(0, B) as b:
                dve.wait_ge(hT_done, b)
                dve.tensor_tensor(hg[:, :].rearrange("p (e r) -> p e r", e=E),
                                  h_all[:, bass.ds(b, 1), :].rearrange("p a (e r) -> p (a e) r", e=E),
                                  gates[:, bass.ds(b, 1), :].rearrange("p a e -> p (a e)").unsqueeze(2)
                                  .broadcast_to([P, E, R0]), ALU.mult).then_inc(gated, 1)
                dve.wait_ge(hT_high, b + 1)
                dve.tensor_tensor(HL, PP[0][:, 0:P], f32(HH), ALU.subtract).then_inc(hT_split, 1)
                dve.wait_ge(lora_done, b + 1)
                row = resid[:, bass.ds(b, 1), :].rearrange("p a d -> p (a d)")
                dve.tensor_tensor(row, SP[0][:, 0:DM], row, ALU.add).then_inc(added, 1)


def lora_layer(nc, sem, v, name, a_rows, rank, b_of, id_at, scaling, wbase, out):
    resid, xTr, XH, XL, WH, WL, ident = (v[k] for k in ("resid", "xTr", "XH", "XL", "WH", "WL", "ident"))
    SP, PP, MA, MB = v["SP"], v["PP"], v["MA"], v["MB"]
    Araw = v["Kraw"]
    Braw = v["Vraw"][:, 0:KC, :].rearrange("p a b -> p (a b)")
    AH, AL = (v[k][:, :].rearrange("p (c r) -> p c r", c=KC) for k in ("QTH", "QTL"))
    BH, BL = v["PH"][:, 0, :], v["PL"][:, 0, :]
    xs, xo, y = v["S"][:, 0, 0:DM], v["S"][:, 1, 0:DM], v["S"][:, 2, 0:DM]
    LH, LL = v["OH"][:, 0:T], v["OL"][:, 0:T]
    names = ("zero", "loaded", "ab_high", "ab_split", "x_copied", "x_biased", "xT", "xT_high", "xT_split", "low",
             "low_high", "low_split", "base", "y", "yT", "kept", "stored")
    (zeroed, loaded, ab_high, ab_split, x_copied, x_biased, xT_done, xT_high, xT_split, low_done,
     low_high, low_split, base_done, y_done, yT_done, kept, stored) = (sem(f"{name}_{n}") for n in names)
    last_layer = out is not None

    def row(b):
        return resid[:, bass.ds(b, 1), :].rearrange("p a d -> p (a d)")

    with nc.Block() as block:
        @block.sync
        def _(sp):
            sp.wait_ge(zeroed, 2)
            with sp.Fori(0, B) as b:
                wait_apart(sp, ab_split, 2 * b, v["passed"])
                a = sp.value_load(v["idrow"][0:1, bass.ds(b + id_at, 1)], min_val=0, max_val=a_rows.shape[0] - 1)
                sp.dma_start(Araw[:, :, 0:rank],
                             a_rows[bass.ds(a, 1), :, :, :].rearrange("a p c r -> p (a c) r")).then_inc(loaded, 16)
                if last_layer:
                    src = v["b3"][bass.ds(a, 1), :, :].rearrange("a r n -> (a r) n")
                else:
                    src = v["b1"]
                sp.dma_start(Braw[0:rank, :], src).then_inc(loaded, 16)
                if last_layer:
                    sp.wait_ge(y_done, b + 1)
                    sp.dma_start(out[bass.ds(b, 1), :, :].rearrange("a t d -> (a t) d"), y).then_inc(stored, 16)
            if last_layer:
                sp.wait_ge(stored, 16 * B)

        @block.gpsimd
        def _(pool):
            pool.memset(Araw[:, :, :], 0.0).then_inc(zeroed, 1)
            pool.memset(Braw, 0.0).then_inc(zeroed, 1)
            with pool.Fori(0, B) as b:
                wait_apart(pool, loaded, 32 * b + 32, v["passed"])
                wait_apart(pool, base_done, b, v["passed"])
                v["split"](pool, AH, AL, Araw[:, :, :], ab_high, 2 * b + 1).then_inc(ab_split, 1)
                v["split"](pool, BH, BL, Braw, ab_high, 2 * b + 2).then_inc(ab_split, 1)
                if not last_layer:
                    wait_apart(pool, y_done, b + 1, v["passed"])
                    pool.tensor_copy(row(b), y).then_inc(kept, 1)

        @block.scalar
        def _(act):
            with act.Fori(0, B) as b:
                act.wait_ge(y_done, b)
                act.wait_ge(xT_done, b)
                act.activation(xs, row(b), ACT.Copy).then_inc(x_copied, 1)
                act.wait_ge(xT_done, b + 1)
                act.wait_ge(base_done, b)
                act.activation(XH[:, :, :].rearrange("p c t -> p (c t)"), MA[:, :], ACT.Copy).then_inc(xT_high, 1)
                act.wait_ge(low_done, b + 1)
                act.activation(LH, MB[:, 0:T], ACT.Copy, scale=scaling).then_inc(low_high, 1)
                if not last_layer:
                    act.wait_ge(yT_done, b + 1)
                    act.activation(xTr[:, bass.ds(b, 1), :, :].rearrange("p a c t -> p (a c t)"), PP[0][:, :],
                                   ACT.Copy).then_inc(kept, 1)

        @block.vector
        def _(dve):
            with dve.Fori(0, B) as b:
                if last_layer:
                    ge(dve, y_done, b)
                    dve.tensor_tensor(xo, row(b), v["biasb"][:, :], ALU.add).then_inc(x_biased, 1)
                dve.wait_ge(xT_high, b + 1)
                dve.tensor_tensor(XL[:, :, :].rearrange("p c t -> p (c t)"), MA[:, :],
                                  f32(XH[:, :, :]).rearrange("p c t -> p (c t)"), ALU.subtract).then_inc(xT_split, 1)
                dve.wait_ge(low_high, b + 1)
                dve.scalar_tensor_tensor(out=LL, in0=MB[:, 0:T], scalar=scaling, in1=f32(LH), op0=ALU.mult,
                                         op1=ALU.subtract).then_inc(low_split, 1)
                dve.wait_ge(base_done, b + 1)
                if last_layer:
                    dve.wait_ge(x_biased, b + 1)
                    dve.wait_ge(stored, 16 * b)
                    dve.tensor_tensor(y, SP[0][:, 0:DM], xo, ALU.add).then_inc(y_done, 1)
                else:
                    dve.wait_ge(kept, 2 * b)
                    dve.wait_ge(x_copied, b + 1)
                    dve.tensor_tensor(y, SP[0][:, 0:DM], xs, ALU.add).then_inc(y_done, 1)

        @block.tensor
        def _(pe):
            with pe.Fori(0, B) as b:
                pe.wait_ge(x_copied, b + 1)
                for c in range(KC):
                    last = pe.transpose(MA[:, c * T:(c + 1) * T], xs[:, c * P:(c + 1) * P], ident[:, :])
                last.then_inc(xT_done, 1)
                pe.wait_ge(xT_split, b + 1)
                pe.wait_ge(ab_split, 2 * b + 2)
                for c in range(KC):
                    last = matmul3(pe, MB[:, 0:T], (AH[:, c, :], AL[:, c, :]), (XH[:, c, :], XL[:, c, :]), c == 0,
                                   c == KC - 1)
                last.then_inc(low_done, 1)
                pe.wait_ge(y_done, b)
                for c in range(KC):
                    at = wbase + c * DM
                    matmul3(pe, SP[0][:, 0:DM], (XH[:, c, :], XL[:, c, :]), (WH[:, at:at + DM], WL[:, at:at + DM]), c == 0,
                            False)
                pe.wait_ge(low_split, b + 1)
                matmul3(pe, SP[0][:, 0:DM], (LH, LL), (BH, BL), False, True).then_inc(base_done, 1)
                if not last_layer:
                    pe.wait_ge(y_done, b + 1)
                    pe.wait_ge(kept, 2 * b)
                    for c in range(KC):
                        last = pe.transpose(PP[0][:, c * T:(c + 1) * T], y[:, c * P:(c + 1) * P], ident[:, :])
                    last.then_inc(yT_done, 1)


def attention(nc, sem, v):
    (resid, xTr, XH, XL, WH, WL, Wraw, ident, tabs, mask_all, mask, Kraw, Vraw, VH, VL, KTH, KTL, QTH, QTL, rt1, rt2,
     roped, knew, S, PH, PL, OH, OL, squares, ssq, var, rstd, mx, nbias, rsum, rinv, SP, PP, MA, MB, idrow,
     neg_half) = (v[k] for k in (
         "resid xTr XH XL WH WL Wraw ident tabs mask_all mask Kraw Vraw VH VL KTH KTL QTH QTL rt1 rt2 "
         "roped knew S PH PL OH OL squares ssq var rstd mx nbias rsum rinv SP PP MA MB idrow neg_half").split())
    kc, vc, W = v["kc"], v["vc"], v["W"]
    names = ("k_loaded v_loaded mask_loaded w_loaded w_high w_split x_high x_split v_high v_split q_proj kv_proj "
             "kT kT_high kT_split q_stats q_mults q_roped q_var q_rstd kv_read k_mults k_roped k_var k_rstd k_ready "
             "qT qT_high qT_split knT knT_high knT_split scores masked nbias exps rinv probs pT p_high p_split pv "
             "o_high o_split o_proj o_added").split()
    s = dict(zip(names, (sem(f"a_{n}") for n in names)))
    (k_loaded, v_loaded, mask_loaded, w_loaded, w_high, w_split, x_high, x_split, v_high, v_split, q_proj, kv_proj,
     kT_done, kT_high, kT_split, q_stats, q_mults, q_roped, q_var, q_rstd, kv_read, k_mults, k_roped, k_var, k_rstd,
     k_ready, qT_done, qT_high, qT_split, knT_done, knT_high, knT_split, scored, masked, nbias_done, exp_done,
     rinv_done, probs, pT_done, p_high, p_split, pv_done, o_high, o_split, o_proj, o_added) = (s[n] for n in names)
    QW = REP * D
    AHEAD = NPIECE + 1

    def batch_row(b):
        return resid[:, bass.ds(b, 1), :].rearrange("p a d -> p (a d)")

    with nc.Block() as block:
        @block.sync
        def _(sp):
            def load_pages(j, raw, cache, loaded):
                for n in range(NPP):
                    page = sp.value_load(idrow[0:1, bass.ds(2 * B + (j % B) * NPP + n, 1)], min_val=0,
                                         max_val=PAGES - 1)
                    q = n % 4
                    sp.dma_start(raw[PSIZE * q:PSIZE * (q + 1), n // 4, :],
                                 cache[bass.ds((j // B) * PAGES + page, 1), :, :].rearrange("a k d -> (a k) d"))\
                        .then_inc(loaded, 16)

            def load_piece(i):
                p = i + NPIECE
                sp.dma_start(Wraw[:, :], W[bass.ds(p // NPIECE, 1), :, bass.ds((p % NPIECE) * WPIECE, WPIECE)]
                             .rearrange("g p n -> p (g n)")).then_inc(w_loaded, 16)

            def load_mask(j):
                sp.dma_start(mask[:, 0:L], mask_all[:, bass.ds(j % B, 1), :].rearrange("p a n -> p (a n)"))\
                    .then_inc(mask_loaded, 16)

            def loads(i):
                wait_apart(sp, kT_done, i + 1, v["passed"])
                load_pages(i + 1, Kraw, kc, k_loaded)
                ge(sp, w_split, i + 1)
                load_piece(i + AHEAD)
                wait_apart(sp, v_split, i + 1, v["passed"])
                load_pages(i + 1, Vraw, vc, v_loaded)
                ge(sp, masked, REP * i + REP)
                load_mask(i + 1)

            load_pages(0, Kraw, kc, k_loaded)
            load_piece(NPIECE)
            load_pages(0, Vraw, vc, v_loaded)
            load_mask(0)
            with sp.Fori(0, N_IT - 1) as i:
                loads(i)

        @block.gpsimd
        def _(pool):
            def split_x(j):
                wait_apart(pool, kv_proj, j, v["passed"]) if not isinstance(j, int) or j else None
                v["split"](pool, XH[:, :, :], XL[:, :, :], xTr[:, bass.ds(j % B, 1), :, :], x_high, j + 1)\
                    .then_inc(x_split, 1)

            def split_piece(i, count):
                wait_apart(pool, w_loaded, 16 * count, v["passed"])
                c = ((i + 2 * NPIECE) % (2 * NPIECE)) * WPIECE
                v["split"](pool, WH[:, bass.ds(c, WPIECE)], WL[:, bass.ds(c, WPIECE)], Wraw[:, :], w_high, count)\
                    .then_inc(w_split, 1)

            def step(i, last=False):
                wait_apart(pool, v_loaded, 16 * NPP * (i + 1), v["passed"])
                wait_apart(pool, kv_read, i + 1, v["passed"])
                wait_apart(pool, pv_done, KT * i, v["passed"]) if not isinstance(i, int) or i else None
                v["split"](pool, VH[:, :, :], VL[:, :, :], Vraw[:, :, :], v_high, i + 1).then_inc(v_split, 1)
                if not last:
                    ge(pool, o_proj, i - 1)
                    split_piece(i + AHEAD, i + 2)
                for h in range(REP):
                    wait_apart(pool, rinv_done, REP * i + h + 1, v["passed"])
                    pool.tensor_scalar(S[:, h, :], S[:, h, :], rinv[:, h:h + 1], 1.0, ALU.mult, ALU.mult)\
                        .then_inc(probs, 1)
                if not last:
                    norms(i + 1)
                    split_x(i + 2)

            def norms(j):
                wait_apart(pool, q_var, j + 1, v["passed"])
                pool.tensor_tensor(rstd[:, 0:REP], var[:, 0:REP], neg_half[:, 0:REP], ALU.pow).then_inc(q_rstd, 1)
                wait_apart(pool, k_var, j + 1, v["passed"])
                pool.tensor_tensor(rstd[:, REP:REP + 1], var[:, REP:REP + 1], neg_half[:, 0:1], ALU.pow)\
                    .then_inc(k_rstd, 1)

            split_x(0)
            split_piece(NPIECE, 1)
            norms(0)
            split_x(1)
            step(0)
            with pool.Fori(1, N_IT - 1) as i:
                step(i)
            step(N_IT - 1, last=True)

        @block.scalar
        def _(act):
            def q_squares(j):
                act.wait_ge(q_mults, j + 1)
                for h in range(REP):
                    last = act.activation(squares[:, h * D:(h + 1) * D], MA[:, h * D:(h + 1) * D], ACT.Square,
                                          accum_out=ssq[:, h:h + 1])
                last.then_inc(q_stats, 1)

            def kv(j):
                act.wait_ge(k_mults, j + 1)
                ge(act, v_split, j)
                act.activation(Vraw[:, KT - 1, :], MA[:, D:2 * D], ACT.Copy)
                act.activation(squares[:, QW:QW + D], MA[:, 0:D], ACT.Square, accum_out=ssq[:, REP:REP + 1])\
                    .then_inc(kv_read, 1)

            def kT(j):
                act.wait_ge(kT_done, j + 1)
                ge(act, scored, REP * j)
                act.activation(KTH[:, 0:L], MB[:, :], ACT.Copy).then_inc(kT_high, 1)

            def qT(j):
                act.wait_ge(qT_done, j + 1)
                act.activation(QTH[:, :], MB[:, :], ACT.Copy).then_inc(qT_high, 1)

            def knT(j):
                act.wait_ge(knT_done, j + 1)
                act.activation(KTH[:, L:NK], PP[1][:, 0:T], ACT.Copy).then_inc(knT_high, 1)

            def exp(i, h):
                act.wait_ge(nbias_done, REP * i + h + 1)
                act.activation(S[:, h, :], S[:, h, :], ACT.Exp, bias=nbias[:, h:h + 1], scale=rstd[:, h:h + 1],
                               accum_out=rsum[:, h:h + 1]).then_inc(exp_done, 1)

            def pT(i, t):
                act.wait_ge(pT_done, KT * i + t + 1)
                ge(act, pv_done, KT * i + t - 1)
                act.activation(PH[:, t % 2, :], PP[t % 2][:, :], ACT.Copy).then_inc(p_high, 1)

            def o(i):
                act.wait_ge(pv_done, KT * i + KT)
                ge(act, o_proj, i)
                act.activation(OH[:, :], MA[:, :], ACT.Copy).then_inc(o_high, 1)

            def step(i, last=False):
                exp(i, 0)
                exp(i, 1)
                if not last:
                    q_squares(i + 1)
                exp(i, 2)
                exp(i, 3)
                if not last:
                    kv(i + 1)
                    kT(i + 1)
                for t in range(KT):
                    pT(i, t)
                if not last:
                    qT(i + 1)
                    knT(i + 1)
                o(i)

            q_squares(0)
            kv(0)
            kT(0)
            qT(0)
            knT(0)
            step(0)
            with act.Fori(1, N_IT - 1) as i:
                step(i)
            step(N_IT - 1, last=True)

        @block.vector
        def _(dve):
            def rope(j, at, n, src, table, read, summed):
                wide = [P, n, D]
                x3 = src.rearrange("p (h d) -> p h d", h=n)
                a, b, o = (t[:, at:at + n * D].rearrange("p (h d) -> p h d", h=n) for t in (rt1, rt2, roped))
                H = D // 2
                tab = [tabs[:, bass.ds(j % B, 1), table + k, :].broadcast_to(wide) for k in range(2)]
                dve.tensor_tensor(a, x3, tab[0], ALU.mult)
                dve.tensor_tensor(b, x3, tab[1], ALU.mult).then_inc(read, 1)
                dve.wait_ge(read, j + 1)
                dve.tensor_tensor(o[:, :, 0:H], a[:, :, 0:H], b[:, :, H:D], ALU.subtract)
                dve.tensor_tensor(o[:, :, H:D], a[:, :, H:D], b[:, :, 0:H], ALU.add).then_inc(summed, 1)

            def q_rope(j):
                dve.wait_ge(q_proj, j + 1)
                ge(dve, qT_done, j)
                rope(j, 0, REP, MA[:, 0:QW], 0, q_mults, q_roped)

            def q_variance(j):
                dve.wait_ge(q_stats, j + 1)
                dve.tensor_scalar(var[:, 0:REP], ssq[:, 0:REP], D * EPS, None, ALU.add).then_inc(q_var, 1)

            def k_rope(j):
                dve.wait_ge(kv_proj, j + 1)
                rope(j, QW, 1, MA[:, 0:D], 2, k_mults, k_roped)
                dve.wait_ge(kv_read, j + 1)
                dve.tensor_scalar(var[:, REP:REP + 1], ssq[:, REP:REP + 1], 1.0 / D, EPS, ALU.mult, ALU.add)\
                    .then_inc(k_var, 1)

            def k_norm(j):
                dve.wait_ge(k_rstd, j + 1)
                dve.wait_ge(k_roped, j + 1)
                ge(dve, knT_done, j)
                dve.tensor_scalar(knew[:, :], roped[:, QW:QW + D], rstd[:, REP:REP + 1], None, ALU.mult)\
                    .then_inc(k_ready, 1)

            def kT(j):
                dve.wait_ge(kT_high, j + 1)
                dve.tensor_tensor(KTL[:, 0:L], MB[:, :], f32(KTH[:, 0:L]), ALU.subtract).then_inc(kT_split, 1)

            def qT(j):
                dve.wait_ge(qT_high, j + 1)
                dve.tensor_tensor(QTL[:, :], MB[:, :], f32(QTH[:, :]), ALU.subtract).then_inc(qT_split, 1)

            def knT(j):
                dve.wait_ge(knT_high, j + 1)
                dve.tensor_tensor(KTL[:, L:NK], PP[1][:, 0:T], f32(KTH[:, L:NK]), ALU.subtract).then_inc(knT_split, 1)

            def mask_max(i, h):
                dve.wait_ge(mask_loaded, 16 * (i + 1))
                ge(dve, pT_done, KT * i)
                wait_apart(dve, scored, REP * i + h + 1, v["passed"])
                dve.tensor_tensor_reduce(out=S[:, h, :], in0=SP[h % 2][:, 0:NK], in1=mask[:, :], scale=1.0,
                                         scalar=-3e38, op0=ALU.add, op1=ALU.max, accum_out=mx[:, h:h + 1])\
                    .then_inc(masked, 1)
                dve.wait_ge(q_rstd, i + 1)
                dve.wait_ge(masked, REP * i + h + 1)
                dve.scalar_tensor_tensor(out=nbias[:, h:h + 1], in0=mx[:, h:h + 1], scalar=-1.0,
                                         in1=rstd[:, h:h + 1], op0=ALU.mult, op1=ALU.mult).then_inc(nbias_done, 1)

            def inverse(i, h):
                dve.wait_ge(exp_done, REP * i + h + 1)
                dve.reciprocal(rinv[:, h:h + 1], rsum[:, h:h + 1]).then_inc(rinv_done, 1)

            def pT(i, t):
                dve.wait_ge(p_high, KT * i + t + 1)
                dve.tensor_tensor(PL[:, t % 2, :], PP[t % 2][:, :], f32(PH[:, t % 2, :]), ALU.subtract)\
                    .then_inc(p_split, 1)

            def o(i):
                dve.wait_ge(o_high, i + 1)
                dve.tensor_tensor(OL[:, :], MA[:, :], f32(OH[:, :]), ALU.subtract).then_inc(o_split, 1)

            def o_add(i):
                dve.wait_ge(o_proj, i + 1)
                dve.tensor_tensor(batch_row(i % B), MB[:, :], batch_row(i % B), ALU.add).then_inc(o_added, 1)

            def step(i, first=False, last=False):
                mask_max(i, 0)
                mask_max(i, 1)
                inverse(i, 0)
                if not last:
                    q_rope(i + 1)
                mask_max(i, 2)
                inverse(i, 1)
                mask_max(i, 3)
                inverse(i, 2)
                if not last:
                    q_variance(i + 1)
                if not first:
                    o_add(i - 1)
                inverse(i, 3)
                if not last:
                    k_rope(i + 1)
                    kT(i + 1)
                pT(i, 0)
                pT(i, 1)
                pT(i, 2)
                if not last:
                    k_norm(i + 1)
                pT(i, 3)
                pT(i, 4)
                if not last:
                    qT(i + 1)
                    knT(i + 1)
                o(i)

            q_rope(0)
            q_variance(0)
            k_rope(0)
            kT(0)
            k_norm(0)
            qT(0)
            knT(0)
            step(0, first=True)
            with dve.Fori(1, N_IT - 1) as i:
                step(i)
            step(N_IT - 1, last=True)
            o_add(N_IT - 1)

        @block.tensor
        def _(pe):
            def w_half(j):
                return ((j // B) % 2) * WG

            def weights(j, at, n):
                base = w_half(j) + at
                return WH[:, bass.ds(base, n)], WL[:, bass.ds(base, n)]

            def q_project(j):
                pe.wait_ge(x_split, j + 1)
                if not isinstance(j, int) or j:
                    ge(pe, w_split, j)
                ge(pe, o_split, j - 1)
                for c in range(KC):
                    last = matmul3(pe, MA[:, :], (XH[:, c, :], XL[:, c, :]), weights(j, W_Q + c * QW, QW), c == 0,
                                   c == KC - 1)
                last.then_inc(q_proj, 1)

            def kv_project(j):
                pe.wait_ge(q_stats, j + 1)
                pe.wait_ge(q_mults, j + 1)
                for c in range(KC):
                    last = matmul3(pe, MA[:, 0:2 * D], (XH[:, c, :], XL[:, c, :]), weights(j, W_KV + c * 2 * D, 2 * D),
                                   c == 0, c == KC - 1)
                last.then_inc(kv_proj, 1)

            def k_transpose(j):
                pe.wait_ge(k_loaded, 16 * NPP * (j + 1))
                ge(pe, o_added, j - 1)
                if isinstance(j, int) and j == 1:
                    pe.wait_ge(qT_split, 1)
                for t in range(L // P):
                    last = pe.transpose(MB[:, t * P:(t + 1) * P], Kraw[:, t, :], ident[:, :])
                last.then_inc(kT_done, 1)

            def q_transpose(j):
                pe.wait_ge(q_roped, j + 1)
                pe.wait_ge(kT_split, j + 1)
                for h in range(REP):
                    last = pe.transpose(MB[:, h * T:(h + 1) * T], roped[:, h * D:(h + 1) * D], ident[:, :])
                last.then_inc(qT_done, 1)

            def kn_transpose(j):
                pe.wait_ge(k_ready, j + 1)
                ge(pe, p_split, KT * (j - 1) + 4)
                pe.transpose(PP[1][:, 0:T], knew[:, :], ident[:, :]).then_inc(knT_done, 1)

            def score(i, h):
                if h == 0:
                    pe.wait_ge(qT_split, i + 1)
                    pe.wait_ge(kT_split, i + 1)
                    pe.wait_ge(knT_split, i + 1)
                ge(pe, masked, REP * i + h - 1)
                qs = QTH[:, h * T:(h + 1) * T], QTL[:, h * T:(h + 1) * T]
                matmul3(pe, SP[h % 2][:, 0:L], qs, (KTH[:, 0:L], KTL[:, 0:L]), True, True)
                matmul3(pe, SP[h % 2][:, L:NK], qs, (KTH[:, L:NK], KTL[:, L:NK]), True, True).then_inc(scored, 1)

            def p_transpose(i, t):
                if t == 0:
                    pe.wait_ge(probs, REP * i + REP)
                if t == 1:
                    pe.wait_ge(knT_split, i + 1)
                ge(pe, p_split, KT * i + t - (1 if t else 0))
                for h in range(REP):
                    last = pe.transpose(PP[t % 2][:, h * T:(h + 1) * T], S[:, h, t * P:(t + 1) * P], ident[:, :])
                last.then_inc(pT_done, 1)

            def pv(i, t, last_step=False):
                pe.wait_ge(p_split, KT * i + t + 1)
                if t == 0:
                    pe.wait_ge(v_split, i + 1)
                    if not last_step:
                        pe.wait_ge(kv_read, i + 2)
                        pe.wait_ge(k_mults, i + 2)
                    else:
                        pe.wait_ge(o_split, i)
                matmul3(pe, MA[:, :], (VH[:, t, :], VL[:, t, :]), (PH[:, t % 2, :], PL[:, t % 2, :]), t == 0,
                        t == KT - 1).then_inc(pv_done, 1)

            def o_project(i):
                pe.wait_ge(o_split, i + 1)
                ge(pe, qT_split, i + 1)
                for h in range(REP):
                    last = matmul3(pe, MB[:, :], (OH[:, h * T:(h + 1) * T], OL[:, h * T:(h + 1) * T]),
                                   weights(i, W_O + h * DM, DM), h == 0, h == REP - 1)
                last.then_inc(o_proj, 1)

            def step(i, first=False, last=False):
                score(i, 0)
                score(i, 1)
                if not last:
                    q_project(i + 1)
                score(i, 2)
                score(i, 3)
                if not first:
                    o_project(i - 1)
                if not last:
                    kv_project(i + 1)
                    k_transpose(i + 1)
                p_transpose(i, 0)
                for t in range(KT):
                    if t + 1 < KT:
                        p_transpose(i, t + 1)
                    elif not last:
                        q_transpose(i + 1)
                        kn_transpose(i + 1)
                    pv(i, t, last)

            q_project(0)
            kv_project(0)
            k_transpose(0)
            q_transpose(0)
            kn_transpose(0)
            step(0, first=True)
            with pe.Fori(1, N_IT - 1) as i:
                step(i)
            step(N_IT - 1, last=True)
            o_project(N_IT - 1)


def kernel(**inputs):
    import concourse.bacc as bacc
    from concourse.bass_utils import run_bass_kernel_spmd

    a = {k: np.asarray(x) for k, x in inputs.items()}

    def chunks(w):
        return w.T.reshape(-1, P, w.shape[0]).transpose(1, 0, 2)

    f = np.float32
    W = np.zeros((HK + 2, P, WG), f)
    W[0, :, W_BASE0:W_AR] = chunks(a["L0_cond_W"]).reshape(P, -1)
    ar = np.concatenate([a["L0_cond_A"].reshape(E * R0, DM), a["L0_cond_Wr"]], 0)
    W[0, :, W_AR:W_AR + KC * AR] = chunks(ar).reshape(P, -1)
    W[0, :, W_BASE1:] = chunks(a["L1_cond_W"]).reshape(P, -1)
    W[HK + 1, :, W_BASE3:] = chunks(a["L3_cond_W"]).reshape(P, -1)
    for g in range(HK):
        rows = slice(g * REP * D, (g + 1) * REP * D)
        kv = np.concatenate([a["L2_cond_Wk"][g * D:(g + 1) * D], a["L2_cond_Wv"][g * D:(g + 1) * D]], 0)
        W[g + 1, :, W_Q:W_KV] = chunks(a["L2_cond_Wq"][rows]).reshape(P, -1)
        W[g + 1, :, W_KV:W_O] = chunks(kv).reshape(P, -1)
        W[g + 1, :, W_O:] = a["L2_cond_Wo"][:, rows].T.reshape(REP, D, DM).transpose(1, 0, 2).reshape(P, -1)
    half_pow = (10000.0 ** (np.arange(0, D, 2) / D)).astype(f)
    arrays = {
        "x": np.ascontiguousarray(a["x"]),
        "xT": np.ascontiguousarray(a["x"].reshape(B, T, KC, P).transpose(3, 0, 2, 1)),
        "W": W,
        "a1": np.ascontiguousarray(a["L1_cond_lora_A"].reshape(-1, KC, P, R1).transpose(0, 2, 1, 3)),
        "b1": np.ascontiguousarray(a["L1_cond_lora_B_w"].T),
        "a3": np.ascontiguousarray(a["L3_cond_lora_As"].reshape(-1, KC, P, R3).transpose(0, 2, 1, 3)),
        "b3": np.ascontiguousarray(a["L3_cond_lora_Bs"]),
        "bcat0": np.ascontiguousarray(a["L0_cond_B"].transpose(0, 2, 1).reshape(E * R0, DM)),
        "bias3": np.ascontiguousarray(a["L3_cond_b"]),
        "kc": np.ascontiguousarray(a["L2_cond_k_cache"].transpose(2, 0, 1, 3)).reshape(HK * PAGES, PSIZE, D),
        "vc": np.ascontiguousarray(a["L2_cond_v_cache"].transpose(2, 0, 1, 3)).reshape(HK * PAGES, PSIZE, D),
        "q_w": np.ascontiguousarray(a["L2_cond_q_norm_w"]),
        "k_w": np.ascontiguousarray(a["L2_cond_k_norm_w"]),
        "inv_freq": f(1) / half_pow,
        "ids": np.concatenate([a["itok_B_0_2"], a["itok_B_0_23"], a["itok_Bx16_0_63"].reshape(-1),
                               a["itok_B_207_1644"], a["itok_B_0_7"]]),
    }
    nc = bacc.Bacc("TRN2", target_bir_lowering=False, num_devices=1)
    args = {k: nc.dram_tensor(f"in_{k}", x.shape, mybir.dt.from_np(x.dtype), kind="ExternalInput").ap()
            for k, x in arrays.items()}
    out = nc.dram_tensor("out_0", (B, T, DM), FP32, kind="ExternalOutput").ap()
    build(nc, out=out, **args)
    r = run_bass_kernel_spmd(nc, [{f"in_{k}": x for k, x in arrays.items()}], core_ids=[0])
    return r.results[0]["out_0"]
```

```python
from contextlib import ExitStack

import numpy as np

import concourse.bass as bass
from concourse import mybir

FP32 = mybir.dt.float32
FP32R = mybir.dt.float32r
BF16 = mybir.dt.bfloat16
I32 = mybir.dt.int32
U32 = mybir.dt.uint32
ALU = mybir.AluOpType
ACT = mybir.ActivationFunctionType

B, T, DM = 8, 128, 512
P = 128
KC = DM // P
E, R0 = 8, 16
R1, R3 = 32, 16
HQ, HK, D = 32, 8, 128
REP = HQ // HK
PAGES, PSIZE, NPP = 64, 32, 16
L = NPP * PSIZE
NK = L + T
KT = NK // P
KCT = L // P
N_IT = HK * B
EPS = 1e-6
LANG_BIAS, SCALING0, SCALING1, SCALING3 = 5.0, 2.0, 0.5, 2.0
MASKED = -1e30

WG = 5120
NPIECE = 8
WPIECE = WG // NPIECE
W_Q, W_KV, W_O = 0, KC * REP * D, KC * (REP * D + 2 * D)
W_BASE0, W_AR, W_BASE1, W_BASE3 = 0, KC * DM, W_O, W_O
AR = E * R0 + E

TWO_PI = 2 * np.pi
C1 = 6.28125
C2 = float(np.float32(int((TWO_PI - C1) * 2.0**21) / 2.0**21))
C3 = float(np.float32(TWO_PI - C1 - C2))
ROUND = float(1.5 * 2**23)
PI_BELOW = float(np.float32(3.1415925))


def ge(eng, sem, value):
    if isinstance(value, int) and value <= 0:
        return
    eng.wait_ge(sem, value)


def wait_apart(eng, sem, value, passed):
    eng.wait_ge(sem, value)
    if not isinstance(value, int):
        eng.sem_inc(passed, 1)


def matmul3(pe, out, lhs, rhs, start, stop):
    pe.matmul(out, lhs[0], rhs[0], start=start, stop=False)
    pe.matmul(out, lhs[0], rhs[1], start=False, stop=False)
    return pe.matmul(out, lhs[1], rhs[0], start=False, stop=stop)


def f32(ap):
    return ap.bitcast(FP32)


def build(nc, x, xT, W, a1, b1, a3, b3, bcat0, bias3, kv_cache, table, q_w, k_w, inv_freq, ids, out):
    ctx = ExitStack()
    with ctx:
        def sb(name, shape, dt=FP32):
            return ctx.enter_context(nc.sbuf_tensor(name, shape, dt))

        def sem(name):
            return ctx.enter_context(nc.semaphore(name))

        resid = sb("resid", [P, B, DM])
        xTr = sb("xTr", [P, B, KC, T])
        WH = sb("WH", [P, 2 * WG], FP32R)
        WL = sb("WL", [P, 2 * WG], FP32R)
        Wraw = sb("Wraw", [P, WPIECE])
        ident = sb("ident", [P, P])
        tabs = sb("tabs", [P, B, 4, D])
        mask_all = sb("mask_all", [P, B, L], BF16)
        mask = sb("mask", [P, NK], BF16)
        idrow = sb("idrow", [1, 2 * B], I32)
        key_rows = sb("key_rows", [P, N_IT * KCT], U32)
        rows = sb("rows", [P, KCT], U32)
        biasb = sb("biasb", [P, DM])
        neg_half = sb("neg_half", [P, 8])
        XH = sb("XH", [P, KC, T], FP32R)
        XL = sb("XL", [P, KC, T], FP32R)
        KV = sb("KV", [P, KT, 2 * D])
        VH = sb("VH", [P, KT, D], FP32R)
        VL = sb("VL", [P, KT, D], FP32R)
        KTH = sb("KTH", [P, NK], FP32R)
        KTL = sb("KTL", [P, NK], FP32R)
        QTH = sb("QTH", [P, REP * T], FP32R)
        QTL = sb("QTL", [P, REP * T], FP32R)
        rt1 = sb("rt1", [P, (REP + 1) * D])
        rt2 = sb("rt2", [P, (REP + 1) * D])
        roped = sb("roped", [P, (REP + 1) * D])
        knew = sb("knew", [P, D])
        S = sb("S", [P, REP, NK])
        PH = sb("PH", [P, 3, REP * T], FP32R)
        PL = sb("PL", [P, 3, REP * T], FP32R)
        OH = sb("OH", [P, REP * T], FP32R)
        OL = sb("OL", [P, REP * T], FP32R)
        squares = sb("squares", [P, (REP + 1) * D], BF16)
        ssq = sb("ssq", [P, REP + 1])
        var = sb("var", [P, REP + 1])
        rstd = sb("rstd", [P, REP + 1])
        mx = sb("mx", [P, REP])
        nbias = sb("nbias", [P, REP])
        rsum = sb("rsum", [P, REP])
        rinv = sb("rinv", [P, REP])

        SP = [ctx.enter_context(nc.psum_tensor(f"SP{i}", [P, 1024], FP32)) for i in range(2)]
        PP = [ctx.enter_context(nc.psum_tensor(f"PP{i}", [P, 512], FP32)) for i in range(2)]
        MA = ctx.enter_context(nc.psum_tensor("MA", [P, 512], FP32))
        MB = ctx.enter_context(nc.psum_tensor("MB", [P, 512], FP32))

        def wcol(piece):
            return ((piece + NPIECE) % (2 * NPIECE)) * WPIECE

        passed = sem("passed")

        def piece_col(i):
            return ((i + 2 * NPIECE) % (2 * NPIECE)) * WPIECE

        def split(eng, hi, lo, src, hi_done, count):
            eng.tensor_scalar(hi, src, 1.0, 1.0, ALU.mult, ALU.mult).then_inc(hi_done, 1)
            wait_apart(eng, hi_done, count, passed)
            return eng.tensor_tensor(lo, src, f32(hi), ALU.subtract)

        def low_part(lo, hi, src):
            return nc.gpsimd.tensor_tensor(lo, src, f32(hi), ALU.subtract)

        setup(nc, sem, locals())
        layer0(nc, sem, locals())
        lora_layer(nc, sem, locals(), "l1", a1, R1, lambda b: b1, 0, SCALING1, (W_BASE1 + WG), None)
        attention(nc, sem, locals())
        lora_layer(nc, sem, locals(), "l3", a3, R3, lambda b: b3[b, :, :], B, SCALING3, W_BASE3, out)


def setup(nc, sem, v):
    ident, tabs, mask_all, mask, neg_half, WH, WL, Wraw = (
        v[k] for k in ("ident", "tabs", "mask_all", "mask", "neg_half", "WH", "WL", "Wraw"))
    ang, turns, red = (v["S"][:, i, 0:B * D // 2].rearrange("p (b f) -> p b f", b=B) for i in range(3))
    cosv = v["S"][:, 3, 0:B * D // 2].rearrange("p (b f) -> p b f", b=B)
    sinv = v["rt2"][:, 0:B * D // 2].rearrange("p (b f) -> p b f", b=B)
    redc = v["roped"][:, 0:B * D // 2].rearrange("p (b f) -> p b f", b=B)
    keyno = v["rt1"][:, 0:L]
    invf = v["knew"][:, 0:D // 2]
    qw, kw = v["rt1"][:, 512:640], v["KV"][:, 0, 0:D]
    seqi = v["KV"][:, 1, 0:B].bitcast(I32)
    seqf, pos, tokno, key_in_page = (v["KV"][:, 2, 16 * i:16 * i + B] for i in range(4))
    pages_i = v["KV"][:, 3, 0:B * KCT].bitcast(I32)
    pages, first_rows = (v["KV"][:, 4, 32 * i:32 * i + B * KCT] for i in range(2))
    loaded, w_loaded, const, w_high, w_low, step, sin_done, cos_done, tok_in, pages_in = (
        sem(f"setup_{n}") for n in ("loaded", "w_loaded", "const", "w_high", "w_low", "step", "sin", "cos", "tok", "pages"))
    ids = v["ids"]
    n_ids = 2 * B
    with nc.Block() as block:
        @block.sync
        def _(sp):
            for q in range(P // PSIZE):
                sp.dma_start(pages_i[q * PSIZE:(q + 1) * PSIZE, :], v["table"][q, :].partition_broadcast(PSIZE))\
                    .then_inc(pages_in, 16)
            for i in range(NPIECE):
                if i:
                    sp.wait_ge(w_low, i)
                sp.dma_start(Wraw[:, :], v["W"][0, :, i * WPIECE:(i + 1) * WPIECE]).then_inc(w_loaded, 16)
            sp.wait_ge(w_loaded, 16 * NPIECE)
            sp.wait_ge(pages_in, 16 * P // PSIZE)

        @block.scalar
        def _(act):
            for dst, src in (
                (seqi, ids[n_ids:n_ids + B].partition_broadcast(P)),
                (invf, v["inv_freq"].partition_broadcast(P)),
                (qw, v["q_w"].partition_broadcast(P)),
                (kw, v["k_w"].partition_broadcast(P)),
                (v["xTr"][:, :, :, :], v["xT"]),
                (v["resid"][:, :, :], v["x"].rearrange("b t d -> t b d")),
                (v["biasb"][:, :], v["bias3"].partition_broadcast(P)),
                (v["idrow"][:, :], ids[0:n_ids].rearrange("(a n) -> a n", a=1)),
            ):
                act.dma_start(dst, src).then_inc(loaded, 16)
            act.wait_ge(step, 8)
            act.activation(sinv, red, ACT.Sin).then_inc(sin_done, 1)
            act.wait_ge(step, 12)
            act.activation(cosv, redc, ACT.Sin).then_inc(cos_done, 1)
            act.wait_ge(loaded, 16 * 8)

        @block.gpsimd
        def _(pool):
            pool.iota(keyno, pattern=[[1, L]], base=0, channel_multiplier=0,
                      allow_small_or_imprecise_dtypes=True).then_inc(const, 1)
            pool.iota(tokno[:, 0:1], pattern=[[0, 1]], base=0, channel_multiplier=1,
                      allow_small_or_imprecise_dtypes=True).then_inc(const, 1)
            for q in range(P // PSIZE):
                pool.wait_ge(const, 2 + q)
                pool.iota(key_in_page[q * PSIZE:(q + 1) * PSIZE, 0:1], pattern=[[0, 1]], base=0, channel_multiplier=1,
                          allow_small_or_imprecise_dtypes=True).then_inc(const, 1)
            pool.wait_ge(const, 2 + P // PSIZE)
            pool.memset(ident[:, :], 0.0).then_inc(tok_in, 1)
            wait_apart(pool, tok_in, 1, v["passed"])
            pool.affine_select(out=ident[:, :], in_=ident[:, :], compare_op=ALU.not_equal, fill=1.0, base=0,
                               pattern=[[-1, P]], channel_multiplier=1)
            pool.memset(neg_half[:, :], -0.5)
            pool.memset(mask[:, :], 0.0)
            for i in range(NPIECE):
                wait_apart(pool, w_loaded, 16 * (i + 1), v["passed"])
                c = v["wcol"](i)
                v["split"](pool, WH[:, c:c + WPIECE], WL[:, c:c + WPIECE], Wraw[:, :], w_high, i + 1).then_inc(w_low, 1)

        @block.vector
        def _(dve):
            count = [0]

            def done(ins):
                count[0] += 1
                ins.then_inc(step, 1)
                dve.wait_ge(step, count[0])

            half = [P, B, D // 2]
            dve.wait_ge(loaded, 16 * 8)
            dve.wait_ge(const, 2 + P // PSIZE)
            done(dve.tensor_copy(seqf, seqi))
            done(dve.tensor_scalar(pos, seqf, tokno[:, 0:1], None, ALU.add))
            done(dve.tensor_tensor(ang, pos.unsqueeze(2).broadcast_to(half), invf.unsqueeze(1).broadcast_to(half),
                                   ALU.mult))
            done(dve.tensor_scalar(turns, ang, float(1 / TWO_PI), ROUND, ALU.mult, ALU.add))
            done(dve.tensor_scalar(turns, turns, ROUND, None, ALU.subtract))
            done(dve.scalar_tensor_tensor(out=red, in0=turns, scalar=-C1, in1=ang, op0=ALU.mult, op1=ALU.add))
            done(dve.scalar_tensor_tensor(out=ang, in0=turns, scalar=-C2, in1=red, op0=ALU.mult, op1=ALU.add))
            done(dve.scalar_tensor_tensor(out=red, in0=turns, scalar=-C3, in1=ang, op0=ALU.mult, op1=ALU.add))
            done(dve.tensor_scalar(redc, red, float(np.pi / 2), None, ALU.add))
            done(dve.tensor_scalar(turns, redc, PI_BELOW, -TWO_PI, ALU.is_gt, ALU.mult))
            done(dve.tensor_tensor(redc, redc, turns, ALU.add))
            done(dve.tensor_scalar(redc, redc, PI_BELOW, -PI_BELOW, ALU.min, ALU.max))
            dve.wait_ge(sin_done, 1)
            dve.wait_ge(cos_done, 1)
            full = [P, B, 2, D // 2]
            for n, (trig, w) in enumerate(((cosv, qw), (sinv, qw), (cosv, kw), (sinv, kw))):
                dve.tensor_tensor(tabs[:, :, n, :].rearrange("p b (a f) -> p b a f", a=2),
                                  trig.unsqueeze(2).broadcast_to(full),
                                  w.rearrange("p (a f) -> p a f", a=2).unsqueeze(1).broadcast_to(full), ALU.mult)
            dve.wait_ge(pages_in, 16 * P // PSIZE)
            done(dve.tensor_copy(pages, pages_i))
            done(dve.tensor_scalar(first_rows, pages, float(PSIZE), key_in_page[:, 0:1], ALU.mult, ALU.add))
            for g in range(HK):
                dve.tensor_scalar(v["key_rows"][:, g * B * KCT:(g + 1) * B * KCT], first_rows,
                                  float(g * PAGES * PSIZE), None, ALU.add)
            for b in range(B):
                dve.tensor_scalar(mask_all[:, b, :], keyno, seqf[:, b:b + 1], MASKED, ALU.is_ge, ALU.mult)


def layer0(nc, sem, v):
    resid, xTr, XH, XL, WH, WL, Wraw, ident = (v[k] for k in ("resid", "xTr", "XH", "XL", "WH", "WL", "Wraw", "ident"))
    SP, PP, MA, MB = v["SP"], v["PP"], v["MA"], v["MB"]
    NH = E * R0
    h_all = v["S"][:, :, :].rearrange("p a b -> p (a b)")[:, 0:B * NH].rearrange("p (b n) -> p b n", b=B)
    logits = v["rt1"][:, 0:B * E].rearrange("p (b e) -> p b e", b=B)
    small = v["rt2"]
    onehot, gates, g2, top, idf, enum = (
        small[:, 64 * i:64 * i + B * E].rearrange("p (b e) -> p b e", b=B) for i in range(6))
    topi = v["roped"][:, 0:B * E].bitcast(U32).rearrange("p (b e) -> p b e", b=B)
    lang_i = v["roped"][:, 64:64 + B].bitcast(I32)
    lang, diff, ediff, esum, w0, w1 = (v["roped"][:, 128 + 16 * i:128 + 16 * i + B] for i in range(6))
    hg = v["knew"]
    BH, BL = v["PH"][:, 0, :], v["PL"][:, 0, :]
    Braw = v["KV"][:, :, :].rearrange("p a b -> p (a b)")[:, 0:DM]
    HH, HL = v["OH"][:, 0:NH], v["OL"][:, 0:NH]
    names = ("x_high", "x_split", "w_loaded", "w_high", "w_low", "base_done", "read", "loaded", "b_high", "b_split",
             "enum", "step", "exp", "gated", "hT", "hT_high", "hT_split", "lora_done", "added")
    (x_high, x_split, w_loaded, w_high, w_low, base_done, read, loaded, b_high, b_split,
     enum_done, step, exp_done, gated, hT_done, hT_high, hT_split, lora_done, added) = (sem(f"l0_{n}") for n in names)
    n_ids = 2 * B
    w = WG
    with nc.Block() as block:
        @block.sync
        def _(sp):
            sp.dma_start(lang_i, v["ids"][n_ids + B:n_ids + 2 * B].partition_broadcast(P)).then_inc(loaded, 16)
            sp.dma_start(Braw, v["bcat0"]).then_inc(loaded, 16)
            for i in range(NPIECE):
                if i:
                    sp.wait_ge(w_low, i)
                sp.dma_start(Wraw[:, :], v["W"][1, :, i * WPIECE:(i + 1) * WPIECE]).then_inc(w_loaded, 16)
            sp.wait_ge(loaded, 32)

        @block.gpsimd
        def _(pool):
            pool.iota(enum, pattern=[[0, B], [1, E]], base=0, channel_multiplier=0,
                      allow_small_or_imprecise_dtypes=True).then_inc(enum_done, 1)
            wait_apart(pool, loaded, 32, v["passed"])
            v["split"](pool, BH, BL, Braw, b_high, 1).then_inc(b_split, 1)
            with pool.Fori(0, B) as b:
                wait_apart(pool, x_high, b + 1, v["passed"])
                v["low_part"](XL[:, :, :], XH[:, :, :], xTr[:, bass.ds(b, 1), :, :]).then_inc(x_split, 1)
                wait_apart(pool, w_high, b + 1, v["passed"])
                v["low_part"](WL[:, bass.ds(b * WPIECE, WPIECE)], WH[:, bass.ds(b * WPIECE, WPIECE)], Wraw[:, :])\
                    .then_inc(w_low, 1)

        @block.tensor
        def _(pe):
            with pe.Fori(0, B) as b:
                pe.wait_ge(x_split, b + 1)
                pe.wait_ge(read, 2 * b)
                for c in range(KC):
                    base = w + W_BASE0 + c * DM
                    matmul3(pe, SP[0][:, 0:DM], (XH[:, c, :], XL[:, c, :]), (WH[:, base:base + DM], WL[:, base:base + DM]),
                            c == 0, c == KC - 1)
                for c in range(KC):
                    ar = w + W_AR + c * AR
                    last = matmul3(pe, SP[1][:, 0:AR], (XH[:, c, :], XL[:, c, :]), (WH[:, ar:ar + AR], WL[:, ar:ar + AR]),
                                   c == 0, c == KC - 1)
                last.then_inc(base_done, 1)
            pe.wait_ge(b_split, 1)
            with pe.Fori(0, B) as b:
                pe.wait_ge(gated, b + 1)
                pe.transpose(PP[0][:, 0:P], hg[:, :], ident[:, :]).then_inc(hT_done, 1)
                pe.wait_ge(hT_split, b + 1)
                pe.wait_ge(added, b)
                matmul3(pe, SP[0][:, 0:DM], (HH, HL), (BH, BL), True, True).then_inc(lora_done, 1)

        @block.scalar
        def _(act):
            with act.Fori(0, B) as b:
                act.wait_ge(base_done, b)
                act.activation(XH[:, :, :].rearrange("p c t -> p (c t)"),
                               xTr[:, bass.ds(b, 1), :, :].rearrange("p a c t -> p (a c t)"), ACT.Copy)\
                    .then_inc(x_high, 1)
                act.wait_ge(w_loaded, 16 * b + 16)
                act.activation(WH[:, bass.ds(b * WPIECE, WPIECE)], Wraw[:, :], ACT.Copy).then_inc(w_high, 1)
            act.wait_ge(step, 5)
            act.activation(ediff, diff, ACT.Exp).then_inc(exp_done, 1)
            with act.Fori(0, B) as b:
                act.wait_ge(hT_done, b + 1)
                act.activation(HH, PP[0][:, 0:P], ACT.Copy).then_inc(hT_high, 1)

        @block.vector
        def _(dve):
            with dve.Fori(0, B) as b:
                dve.wait_ge(base_done, b + 1)
                row = resid[:, bass.ds(b, 1), :].rearrange("p a d -> p (a d)")
                dve.tensor_tensor(row, SP[0][:, 0:DM], row, ALU.add).then_inc(read, 1)
                hl = h_all[:, bass.ds(b, 1), :].rearrange("p a d -> p (a d)")
                dve.tensor_copy(hl, SP[1][:, 0:NH])
                dve.tensor_copy(logits[:, bass.ds(b, 1), :].rearrange("p a d -> p (a d)"), SP[1][:, NH:AR])\
                    .then_inc(read, 1)
            dve.wait_ge(read, 2 * B)
            dve.wait_ge(loaded, 32)
            dve.wait_ge(enum_done, 1)
            count = [0]

            def done(ins):
                count[0] += 1
                ins.then_inc(step, 1)
                dve.wait_ge(step, count[0])

            all8 = [P, B, E]
            done(dve.tensor_copy(lang, lang_i))
            done(dve.tensor_tensor(onehot, enum, lang.unsqueeze(2).broadcast_to(all8), ALU.is_equal))
            done(dve.scalar_tensor_tensor(out=logits, in0=onehot, scalar=LANG_BIAS, in1=logits, op0=ALU.mult,
                                          op1=ALU.add))
            for b in range(B):
                ins = dve.max(top[:, b, :], logits[:, b, :])
            done(ins)
            done(dve.tensor_tensor(diff, top[:, :, 1], top[:, :, 0], ALU.subtract))
            for b in range(B):
                ins = dve.max_index(topi[:, b, :], top[:, b, :], logits[:, b, :])
            done(ins)
            dve.tensor_copy(idf, topi)
            dve.wait_ge(exp_done, 1)
            done(dve.tensor_scalar(esum, ediff, 1.0, None, ALU.add))
            done(dve.reciprocal(w0, esum))
            done(dve.tensor_tensor(w1, w0, ediff, ALU.mult))
            dve.tensor_tensor(gates, enum, idf[:, :, 0:1].broadcast_to(all8), ALU.is_equal)
            done(dve.tensor_tensor(g2, enum, idf[:, :, 1:2].broadcast_to(all8), ALU.is_equal))
            done(dve.tensor_tensor(gates, gates, w0.unsqueeze(2).broadcast_to(all8), ALU.mult))
            done(dve.tensor_tensor(g2, g2, w1.unsqueeze(2).broadcast_to(all8), ALU.mult))
            done(dve.tensor_tensor(gates, gates, g2, ALU.add))
            done(dve.tensor_scalar(gates, gates, SCALING0, None, ALU.mult))
            with dve.Fori(0, B) as b:
                dve.wait_ge(hT_done, b)
                dve.tensor_tensor(hg[:, :].rearrange("p (e r) -> p e r", e=E),
                                  h_all[:, bass.ds(b, 1), :].rearrange("p a (e r) -> p (a e) r", e=E),
                                  gates[:, bass.ds(b, 1), :].rearrange("p a e -> p (a e)").unsqueeze(2)
                                  .broadcast_to([P, E, R0]), ALU.mult).then_inc(gated, 1)
                dve.wait_ge(hT_high, b + 1)
                dve.tensor_tensor(HL, PP[0][:, 0:P], f32(HH), ALU.subtract).then_inc(hT_split, 1)
                dve.wait_ge(lora_done, b + 1)
                row = resid[:, bass.ds(b, 1), :].rearrange("p a d -> p (a d)")
                dve.tensor_tensor(row, SP[0][:, 0:DM], row, ALU.add).then_inc(added, 1)


def lora_layer(nc, sem, v, name, a_rows, rank, b_of, id_at, scaling, wbase, out):
    resid, xTr, XH, XL, WH, WL, ident = (v[k] for k in ("resid", "xTr", "XH", "XL", "WH", "WL", "ident"))
    SP, PP, MA, MB = v["SP"], v["PP"], v["MA"], v["MB"]
    kv = v["KV"][:, :, :].rearrange("p a b -> p (a b)")
    Araw = kv[:, 0:KC * P].rearrange("p (c r) -> p c r", c=KC)
    Braw = kv[:, KC * P:KC * P + DM]
    AH, AL = (v[k][:, :].rearrange("p (c r) -> p c r", c=KC) for k in ("QTH", "QTL"))
    BH, BL = v["PH"][:, 0, :], v["PL"][:, 0, :]
    xs, xo, y = v["S"][:, 0, 0:DM], v["S"][:, 1, 0:DM], v["S"][:, 2, 0:DM]
    LH, LL = v["OH"][:, 0:T], v["OL"][:, 0:T]
    names = ("zero", "loaded", "ab_high", "ab_split", "x_copied", "x_biased", "xT", "xT_high", "xT_split", "low",
             "low_high", "low_split", "base", "y", "yT", "kept", "stored")
    (zeroed, loaded, ab_high, ab_split, x_copied, x_biased, xT_done, xT_high, xT_split, low_done,
     low_high, low_split, base_done, y_done, yT_done, kept, stored) = (sem(f"{name}_{n}") for n in names)
    last_layer = out is not None

    def row(b):
        return resid[:, bass.ds(b, 1), :].rearrange("p a d -> p (a d)")

    with nc.Block() as block:
        @block.sync
        def _(sp):
            sp.wait_ge(zeroed, 2)
            with sp.Fori(0, B) as b:
                wait_apart(sp, ab_split, 2 * b, v["passed"])
                a = sp.value_load(v["idrow"][0:1, bass.ds(b + id_at, 1)], min_val=0, max_val=a_rows.shape[0] - 1)
                sp.dma_start(Araw[:, :, 0:rank],
                             a_rows[bass.ds(a, 1), :, :, :].rearrange("a p c r -> p (a c) r")).then_inc(loaded, 16)
                if last_layer:
                    src = v["b3"][bass.ds(a, 1), :, :].rearrange("a r n -> (a r) n")
                else:
                    src = v["b1"]
                sp.dma_start(Braw[0:rank, :], src).then_inc(loaded, 16)
                if last_layer:
                    sp.wait_ge(y_done, b + 1)
                    sp.dma_start(out[bass.ds(b, 1), :, :].rearrange("a t d -> (a t) d"), y).then_inc(stored, 16)
            if last_layer:
                sp.wait_ge(stored, 16 * B)

        @block.gpsimd
        def _(pool):
            pool.memset(Araw[:, :, :], 0.0).then_inc(zeroed, 1)
            pool.memset(Braw, 0.0).then_inc(zeroed, 1)
            with pool.Fori(0, B) as b:
                wait_apart(pool, loaded, 32 * b + 32, v["passed"])
                wait_apart(pool, base_done, b, v["passed"])
                v["split"](pool, AH, AL, Araw[:, :, :], ab_high, 2 * b + 1).then_inc(ab_split, 1)
                v["split"](pool, BH, BL, Braw, ab_high, 2 * b + 2).then_inc(ab_split, 1)
                if not last_layer:
                    wait_apart(pool, y_done, b + 1, v["passed"])
                    pool.tensor_copy(row(b), y).then_inc(kept, 1)

        @block.scalar
        def _(act):
            with act.Fori(0, B) as b:
                act.wait_ge(y_done, b)
                act.wait_ge(xT_done, b)
                act.activation(xs, row(b), ACT.Copy).then_inc(x_copied, 1)
                act.wait_ge(xT_done, b + 1)
                act.wait_ge(base_done, b)
                act.activation(XH[:, :, :].rearrange("p c t -> p (c t)"), MA[:, :], ACT.Copy).then_inc(xT_high, 1)
                act.wait_ge(low_done, b + 1)
                act.activation(LH, MB[:, 0:T], ACT.Copy, scale=scaling).then_inc(low_high, 1)
                if not last_layer:
                    act.wait_ge(yT_done, b + 1)
                    act.activation(xTr[:, bass.ds(b, 1), :, :].rearrange("p a c t -> p (a c t)"), PP[0][:, :],
                                   ACT.Copy).then_inc(kept, 1)

        @block.vector
        def _(dve):
            with dve.Fori(0, B) as b:
                if last_layer:
                    ge(dve, y_done, b)
                    dve.tensor_tensor(xo, row(b), v["biasb"][:, :], ALU.add).then_inc(x_biased, 1)
                dve.wait_ge(xT_high, b + 1)
                dve.tensor_tensor(XL[:, :, :].rearrange("p c t -> p (c t)"), MA[:, :],
                                  f32(XH[:, :, :]).rearrange("p c t -> p (c t)"), ALU.subtract).then_inc(xT_split, 1)
                dve.wait_ge(low_high, b + 1)
                dve.scalar_tensor_tensor(out=LL, in0=MB[:, 0:T], scalar=scaling, in1=f32(LH), op0=ALU.mult,
                                         op1=ALU.subtract).then_inc(low_split, 1)
                dve.wait_ge(base_done, b + 1)
                if last_layer:
                    dve.wait_ge(x_biased, b + 1)
                    dve.wait_ge(stored, 16 * b)
                    dve.tensor_tensor(y, SP[0][:, 0:DM], xo, ALU.add).then_inc(y_done, 1)
                else:
                    dve.wait_ge(kept, 2 * b)
                    dve.wait_ge(x_copied, b + 1)
                    dve.tensor_tensor(y, SP[0][:, 0:DM], xs, ALU.add).then_inc(y_done, 1)

        @block.tensor
        def _(pe):
            with pe.Fori(0, B) as b:
                pe.wait_ge(x_copied, b + 1)
                for c in range(KC):
                    last = pe.transpose(MA[:, c * T:(c + 1) * T], xs[:, c * P:(c + 1) * P], ident[:, :])
                last.then_inc(xT_done, 1)
                pe.wait_ge(xT_split, b + 1)
                pe.wait_ge(ab_split, 2 * b + 2)
                for c in range(KC):
                    last = matmul3(pe, MB[:, 0:T], (AH[:, c, :], AL[:, c, :]), (XH[:, c, :], XL[:, c, :]), c == 0,
                                   c == KC - 1)
                last.then_inc(low_done, 1)
                pe.wait_ge(y_done, b)
                for c in range(KC):
                    at = wbase + c * DM
                    matmul3(pe, SP[0][:, 0:DM], (XH[:, c, :], XL[:, c, :]), (WH[:, at:at + DM], WL[:, at:at + DM]), c == 0,
                            False)
                pe.wait_ge(low_split, b + 1)
                matmul3(pe, SP[0][:, 0:DM], (LH, LL), (BH, BL), False, True).then_inc(base_done, 1)
                if not last_layer:
                    pe.wait_ge(y_done, b + 1)
                    pe.wait_ge(kept, 2 * b)
                    for c in range(KC):
                        last = pe.transpose(PP[0][:, c * T:(c + 1) * T], y[:, c * P:(c + 1) * P], ident[:, :])
                    last.then_inc(yT_done, 1)


def attention(nc, sem, v):
    (resid, xTr, XH, XL, WH, WL, Wraw, ident, tabs, mask_all, mask, KV, key_rows, rows, VH, VL, KTH, KTL, QTH, QTL, rt1, rt2,
     roped, knew, S, PH, PL, OH, OL, squares, ssq, var, rstd, mx, nbias, rsum, rinv, SP, PP, MA, MB, idrow,
     neg_half) = (v[k] for k in (
         "resid xTr XH XL WH WL Wraw ident tabs mask_all mask KV key_rows rows VH VL KTH KTL QTH QTL rt1 rt2 "
         "roped knew S PH PL OH OL squares ssq var rstd mx nbias rsum rinv SP PP MA MB idrow neg_half").split())
    kv_cache, W = v["kv_cache"], v["W"]
    names = ("rows_copied kv_loaded mask_loaded w_loaded w_high w_split x_high x_split v_high v_split q_proj kv_proj "
             "kT kT_high kT_split q_stats q_mults q_roped q_var rstd_done kv_read k_mults k_roped k_var k_ready "
             "qT qT_high qT_split knT knT_high knT_split scores masked nbias exps rinv probs pT p_high p_split pv "
             "o_high o_split o_proj o_added").split()
    s = dict(zip(names, (sem(f"a_{n}") for n in names)))
    (rows_copied, kv_loaded, mask_loaded, w_loaded, w_high, w_split, x_high, x_split, v_high, v_split, q_proj, kv_proj,
     kT_done, kT_high, kT_split, q_stats, q_mults, q_roped, q_var, rstd_done, kv_read, k_mults, k_roped, k_var,
     k_ready, qT_done, qT_high, qT_split, knT_done, knT_high, knT_split, scored, masked, nbias_done, exp_done,
     rinv_done, probs, pT_done, p_high, p_split, pv_done, o_high, o_split, o_proj, o_added) = (s[n] for n in names)
    QW = REP * D
    pT_banks = [PP[0][:, :], PP[1][:, :], SP[1][:, 0:512], SP[0][:, 0:512], SP[1][:, 512:1024]]
    kv_bank = SP[0][:, 512:512 + 2 * D]
    AHEAD = NPIECE + 1

    def batch_row(b):
        return resid[:, bass.ds(b, 1), :].rearrange("p a d -> p (a d)")

    with nc.Block() as block:
        @block.sync
        def _(sp):
            def load_piece(i):
                p = i + NPIECE
                sp.dma_start(Wraw[:, :], W[bass.ds(p // NPIECE, 1), :, bass.ds((p % NPIECE) * WPIECE, WPIECE)]
                             .rearrange("g p n -> p (g n)")).then_inc(w_loaded, 16)

            def load_mask(j):
                sp.dma_start(mask[:, 0:L], mask_all[:, bass.ds(j % B, 1), :].rearrange("p a n -> p (a n)"))\
                    .then_inc(mask_loaded, 16)

            def loads(i):
                ge(sp, w_split, i + 1)
                load_piece(i + AHEAD)
                ge(sp, masked, REP * i + REP)
                load_mask(i + 1)

            load_piece(NPIECE)
            load_mask(0)
            with sp.Fori(0, N_IT - 1) as i:
                loads(i)

        @block.gpsimd
        def _(pool):
            def split_x(j):
                wait_apart(pool, x_high, j + 1, v["passed"])
                v["low_part"](XL[:, :, :], XH[:, :, :], xTr[:, bass.ds(j % B, 1), :, :]).then_inc(x_split, 1)

            def gather(j):
                pool.tensor_copy(rows[:, :], key_rows[:, bass.ds(j * KCT, KCT)]).then_inc(rows_copied, 1)
                wait_apart(pool, rows_copied, j + 1, v["passed"])
                for t in range(KCT):
                    pool.indirect_dma_start(KV[:, t, :], None, kv_cache,
                                            bass.IndirectOffsetOnAxis(ap=rows[:, t:t + 1], axis=0))\
                        .then_inc(kv_loaded, 16)

            def split_piece(i, count):
                wait_apart(pool, w_high, count, v["passed"])
                c = v["piece_col"](i)
                v["low_part"](WL[:, bass.ds(c, WPIECE)], WH[:, bass.ds(c, WPIECE)], Wraw[:, :]).then_inc(w_split, 1)

            def step(i, last=False):
                wait_apart(pool, v_high, i + 1, v["passed"])
                v["low_part"](VL[:, :, :], VH[:, :, :], KV[:, :, D:2 * D]).then_inc(v_split, 1)
                if not last:
                    wait_apart(pool, kT_done, i + 1, v["passed"])
                    wait_apart(pool, v_split, i + 1, v["passed"])
                    gather(i + 1)
                for h in range(REP):
                    wait_apart(pool, rinv_done, REP * i + h + 1, v["passed"])
                    pool.tensor_scalar(S[:, h, :], S[:, h, :], rinv[:, h:h + 1], 1.0, ALU.mult, ALU.mult)\
                        .then_inc(probs, 1)
                if not last:
                    split_piece(i + AHEAD, i + 2)
                    norms(i + 1)
                    split_x(i + 2)

            def norms(j):
                wait_apart(pool, q_var, j + 1, v["passed"])
                wait_apart(pool, k_var, j + 1, v["passed"])
                pool.tensor_tensor(rstd[:, :], var[:, :], neg_half[:, 0:REP + 1], ALU.pow).then_inc(rstd_done, 1)

            gather(0)
            split_x(0)
            split_piece(NPIECE, 1)
            norms(0)
            split_x(1)
            step(0)
            with pool.Fori(1, N_IT - 1) as i:
                step(i)
            step(N_IT - 1, last=True)

        @block.scalar
        def _(act):
            def q_squares(j):
                act.wait_ge(q_mults, j + 1)
                for h in range(REP):
                    last = act.activation(squares[:, h * D:(h + 1) * D], MA[:, h * D:(h + 1) * D], ACT.Square,
                                          accum_out=ssq[:, h:h + 1])
                last.then_inc(q_stats, 1)

            def kv(j):
                act.wait_ge(k_mults, j + 1)
                ge(act, v_split, j)
                act.activation(KV[:, KT - 1, D:2 * D], kv_bank[:, D:2 * D], ACT.Copy)
                act.activation(squares[:, QW:QW + D], kv_bank[:, 0:D], ACT.Square, accum_out=ssq[:, REP:REP + 1])\
                    .then_inc(kv_read, 1)

            def kT(j):
                act.wait_ge(kT_done, j + 1)
                ge(act, scored, REP * j)
                act.activation(KTH[:, 0:L], MB[:, :], ACT.Copy).then_inc(kT_high, 1)

            def qT(j):
                act.wait_ge(qT_done, j + 1)
                act.activation(QTH[:, :], MB[:, :], ACT.Copy).then_inc(qT_high, 1)

            def knT(j):
                act.wait_ge(knT_done, j + 1)
                act.activation(KTH[:, L:NK], SP[0][:, 512:512 + T], ACT.Copy).then_inc(knT_high, 1)

            def v_split_high(i):
                act.wait_ge(kv_loaded, 16 * KCT * (i + 1))
                act.wait_ge(kv_read, i + 1)
                ge(act, pv_done, KT * i)
                act.activation(VH[:, :, :], KV[:, :, D:2 * D], ACT.Copy).then_inc(v_high, 1)

            def w_split_high(i, count):
                act.wait_ge(w_loaded, 16 * count)
                act.activation(WH[:, bass.ds(v["piece_col"](i), WPIECE)], Wraw[:, :], ACT.Copy).then_inc(w_high, 1)

            def exp(i, h):
                act.wait_ge(nbias_done, REP * i + h + 1)
                act.activation(S[:, h, :], S[:, h, :], ACT.Exp, bias=nbias[:, h:h + 1], scale=rstd[:, h:h + 1],
                               accum_out=rsum[:, h:h + 1]).then_inc(exp_done, 1)

            def pT(i, t):
                act.wait_ge(pT_done, KT * i + t + 1)
                ge(act, pv_done, KT * i + max(t - 2, 0))
                act.activation(PH[:, t % 3, :], pT_banks[t], ACT.Copy).then_inc(p_high, 1)

            def o(i):
                act.wait_ge(pv_done, KT * i + KT)
                ge(act, o_proj, i)
                act.activation(OH[:, :], MA[:, :], ACT.Copy).then_inc(o_high, 1)

            def step(i, last=False):
                v_split_high(i)
                exp(i, 0)
                exp(i, 1)
                if not last:
                    w_split_high(i + AHEAD, i + 2)
                exp(i, 2)
                exp(i, 3)
                if not last:
                    q_squares(i + 1)
                    kv(i + 1)
                    kT(i + 1)
                for t in range(KT):
                    pT(i, t)
                    if t == 1 and not last:
                        qT(i + 1)
                if not last:
                    knT(i + 1)
                o(i)

            w_split_high(NPIECE, 1)
            q_squares(0)
            kv(0)
            kT(0)
            qT(0)
            knT(0)
            step(0)
            with act.Fori(1, N_IT - 1) as i:
                step(i)
            step(N_IT - 1, last=True)

        @block.vector
        def _(dve):
            def x_split_high(j):
                ge(dve, kv_proj, j)
                dve.tensor_copy(XH[:, :, :], xTr[:, bass.ds(j % B, 1), :, :]
                                .rearrange("p a c t -> p (a c) t")).then_inc(x_high, 1)

            def rope_mults(j, at, n, src, table, read):
                wide = [P, n, D]
                x3 = src.rearrange("p (h d) -> p h d", h=n)
                for k, t in enumerate((rt1, rt2)):
                    last = dve.tensor_tensor(t[:, at:at + n * D].rearrange("p (h d) -> p h d", h=n), x3,
                                             tabs[:, bass.ds(j % B, 1), table + k, :].broadcast_to(wide), ALU.mult)
                last.then_inc(read, 1)

            def rope_sums(j, at, n, read, summed):
                a, b, o = (t[:, at:at + n * D].rearrange("p (h d) -> p h d", h=n) for t in (rt1, rt2, roped))
                H = D // 2
                dve.wait_ge(read, j + 1)
                dve.tensor_tensor(o[:, :, 0:H], a[:, :, 0:H], b[:, :, H:D], ALU.subtract)
                dve.tensor_tensor(o[:, :, H:D], a[:, :, H:D], b[:, :, 0:H], ALU.add).then_inc(summed, 1)

            def q_rope_mults(j):
                dve.wait_ge(q_proj, j + 1)
                ge(dve, qT_done, j)
                rope_mults(j, 0, REP, MA[:, 0:QW], 0, q_mults)

            def q_rope_sums(j):
                rope_sums(j, 0, REP, q_mults, q_roped)

            def q_variance(j):
                dve.wait_ge(q_stats, j + 1)
                dve.tensor_scalar(var[:, 0:REP], ssq[:, 0:REP], D * EPS, None, ALU.add).then_inc(q_var, 1)

            def k_rope(j):
                dve.wait_ge(kv_proj, j + 1)
                rope_mults(j, QW, 1, kv_bank[:, 0:D], 2, k_mults)
                rope_sums(j, QW, 1, k_mults, k_roped)
                dve.wait_ge(kv_read, j + 1)
                dve.tensor_scalar(var[:, REP:REP + 1], ssq[:, REP:REP + 1], 1.0 / D, EPS, ALU.mult, ALU.add)\
                    .then_inc(k_var, 1)

            def k_norm(j):
                dve.wait_ge(rstd_done, j + 1)
                dve.wait_ge(k_roped, j + 1)
                ge(dve, knT_done, j)
                dve.tensor_scalar(knew[:, :], roped[:, QW:QW + D], rstd[:, REP:REP + 1], None, ALU.mult)\
                    .then_inc(k_ready, 1)

            def kT(j):
                dve.wait_ge(kT_high, j + 1)
                dve.tensor_tensor(KTL[:, 0:L], MB[:, :], f32(KTH[:, 0:L]), ALU.subtract).then_inc(kT_split, 1)

            def qT(j):
                dve.wait_ge(qT_high, j + 1)
                dve.tensor_tensor(QTL[:, :], MB[:, :], f32(QTH[:, :]), ALU.subtract).then_inc(qT_split, 1)

            def knT(j):
                dve.wait_ge(knT_high, j + 1)
                dve.tensor_tensor(KTL[:, L:NK], SP[0][:, 512:512 + T], f32(KTH[:, L:NK]), ALU.subtract).then_inc(knT_split, 1)

            def mask_max(i, h):
                dve.wait_ge(mask_loaded, 16 * (i + 1))
                ge(dve, pT_done, KT * i)
                wait_apart(dve, scored, REP * i + h + 1, v["passed"])
                dve.tensor_tensor_reduce(out=S[:, h, :], in0=SP[h % 2][:, 0:NK], in1=mask[:, :], scale=1.0,
                                         scalar=-3e38, op0=ALU.add, op1=ALU.max, accum_out=mx[:, h:h + 1])\
                    .then_inc(masked, 1)
                dve.wait_ge(rstd_done, i + 1)
                dve.wait_ge(masked, REP * i + h + 1)
                dve.scalar_tensor_tensor(out=nbias[:, h:h + 1], in0=mx[:, h:h + 1], scalar=-1.0,
                                         in1=rstd[:, h:h + 1], op0=ALU.mult, op1=ALU.mult).then_inc(nbias_done, 1)

            def inverse(i, h):
                dve.wait_ge(exp_done, REP * i + h + 1)
                dve.reciprocal(rinv[:, h:h + 1], rsum[:, h:h + 1]).then_inc(rinv_done, 1)

            def pT(i, t):
                dve.wait_ge(p_high, KT * i + t + 1)
                dve.tensor_tensor(PL[:, t % 3, :], pT_banks[t], f32(PH[:, t % 3, :]), ALU.subtract)\
                    .then_inc(p_split, 1)

            def o(i):
                dve.wait_ge(o_high, i + 1)
                dve.tensor_tensor(OL[:, :], MA[:, :], f32(OH[:, :]), ALU.subtract).then_inc(o_split, 1)

            def o_add(i):
                dve.wait_ge(o_proj, i + 1)
                dve.tensor_tensor(batch_row(i % B), MB[:, :], batch_row(i % B), ALU.add).then_inc(o_added, 1)

            def step(i, first=False, last=False):
                mask_max(i, 0)
                mask_max(i, 1)
                inverse(i, 0)
                mask_max(i, 2)
                inverse(i, 1)
                mask_max(i, 3)
                inverse(i, 2)
                if not last:
                    q_rope_mults(i + 1)
                inverse(i, 3)
                if not last:
                    q_rope_sums(i + 1)
                    q_variance(i + 1)
                if not first:
                    o_add(i - 1)
                if not last:
                    k_rope(i + 1)
                    kT(i + 1)
                pT(i, 0)
                pT(i, 1)
                if not last:
                    qT(i + 1)
                    k_norm(i + 1)
                pT(i, 2)
                pT(i, 3)
                pT(i, 4)
                if not last:
                    knT(i + 1)
                    x_split_high(i + 2)
                o(i)

            x_split_high(0)
            q_rope_mults(0)
            q_rope_sums(0)
            q_variance(0)
            k_rope(0)
            x_split_high(1)
            kT(0)
            k_norm(0)
            qT(0)
            knT(0)
            step(0, first=True)
            with dve.Fori(1, N_IT - 1) as i:
                step(i)
            step(N_IT - 1, last=True)
            o_add(N_IT - 1)

        @block.tensor
        def _(pe):
            def w_half(j):
                return ((j // B) % 2) * WG

            def weights(j, at, n):
                base = w_half(j) + at
                return WH[:, bass.ds(base, n)], WL[:, bass.ds(base, n)]

            def q_project(j, chunks):
                if chunks[0] == 0:
                    pe.wait_ge(x_split, j + 1)
                    ge(pe, w_split, j)
                    ge(pe, o_split, j - 1)
                for c in chunks:
                    last = matmul3(pe, MA[:, :], (XH[:, c, :], XL[:, c, :]), weights(j, W_Q + c * QW, QW), c == 0,
                                   c == KC - 1)
                if chunks[-1] == KC - 1:
                    last.then_inc(q_proj, 1)

            def kv_project(j):
                ge(pe, masked, REP * j - 1)
                for c in range(KC):
                    last = matmul3(pe, kv_bank, (XH[:, c, :], XL[:, c, :]), weights(j, W_KV + c * 2 * D, 2 * D),
                                   c == 0, c == KC - 1)
                last.then_inc(kv_proj, 1)

            def k_transpose(j):
                pe.wait_ge(kv_loaded, 16 * KCT * (j + 1))
                ge(pe, o_added, j - 1)
                if isinstance(j, int) and j == 1:
                    pe.wait_ge(qT_split, 1)
                for t in range(L // P):
                    last = pe.transpose(MB[:, t * P:(t + 1) * P], KV[:, t, 0:D], ident[:, :])
                last.then_inc(kT_done, 1)

            def q_transpose(j):
                pe.wait_ge(q_roped, j + 1)
                pe.wait_ge(kT_split, j + 1)
                for h in range(REP):
                    last = pe.transpose(MB[:, h * T:(h + 1) * T], roped[:, h * D:(h + 1) * D], ident[:, :])
                last.then_inc(qT_done, 1)

            def kn_transpose(j):
                pe.wait_ge(k_ready, j + 1)
                pe.wait_ge(kv_read, j + 1)
                pe.transpose(SP[0][:, 512:512 + T], knew[:, :], ident[:, :]).then_inc(knT_done, 1)

            def score(i, h):
                if h == 0:
                    pe.wait_ge(qT_split, i + 1)
                    pe.wait_ge(kT_split, i + 1)
                    pe.wait_ge(knT_split, i + 1)
                if h < 2:
                    ge(pe, p_split, KT * (i - 1) + 4 + h)
                else:
                    pe.wait_ge(masked, REP * i + h - 1)
                qs = QTH[:, h * T:(h + 1) * T], QTL[:, h * T:(h + 1) * T]
                matmul3(pe, SP[h % 2][:, 0:L], qs, (KTH[:, 0:L], KTL[:, 0:L]), True, True)
                matmul3(pe, SP[h % 2][:, L:NK], qs, (KTH[:, L:NK], KTL[:, L:NK]), True, True).then_inc(scored, 1)

            def p_transpose(i, t):
                if t == 0:
                    pe.wait_ge(probs, REP * i + REP)
                ge(pe, p_split, KT * i)
                for h in range(REP):
                    last = pe.transpose(pT_banks[t][:, h * T:(h + 1) * T], S[:, h, t * P:(t + 1) * P], ident[:, :])
                last.then_inc(pT_done, 1)

            def pv(i, t, last_step=False):
                pe.wait_ge(p_split, KT * i + t + 1)
                if t == 0:
                    pe.wait_ge(v_split, i + 1)
                    if not last_step:
                        pe.wait_ge(q_stats, i + 2)
                    else:
                        pe.wait_ge(o_split, i)
                matmul3(pe, MA[:, :], (VH[:, t, :], VL[:, t, :]), (PH[:, t % 3, :], PL[:, t % 3, :]), t == 0,
                        t == KT - 1).then_inc(pv_done, 1)

            def o_project(i):
                pe.wait_ge(o_split, i + 1)
                ge(pe, qT_split, i + 1)
                for h in range(REP):
                    last = matmul3(pe, MB[:, :], (OH[:, h * T:(h + 1) * T], OL[:, h * T:(h + 1) * T]),
                                   weights(i, W_O + h * DM, DM), h == 0, h == REP - 1)
                last.then_inc(o_proj, 1)

            def step(i, first=False, last=False):
                score(i, 0)
                score(i, 1)
                if not last:
                    q_project(i + 1, (0, 1))
                score(i, 2)
                score(i, 3)
                if not last:
                    q_project(i + 1, (2, 3))
                if not first:
                    o_project(i - 1)
                if not last:
                    kv_project(i + 1)
                    k_transpose(i + 1)
                p_transpose(i, 0)
                p_transpose(i, 1)
                p_transpose(i, 2)
                if not last:
                    q_transpose(i + 1)
                pv(i, 0, last)
                p_transpose(i, 3)
                pv(i, 1, last)
                p_transpose(i, 4)
                pv(i, 2, last)
                if not last:
                    kn_transpose(i + 1)
                pv(i, 3, last)
                pv(i, 4, last)

            q_project(0, range(KC))
            kv_project(0)
            k_transpose(0)
            q_transpose(0)
            kn_transpose(0)
            step(0, first=True)
            with pe.Fori(1, N_IT - 1) as i:
                step(i)
            step(N_IT - 1, last=True)
            o_project(N_IT - 1)


def kernel(**inputs):
    import concourse.bacc as bacc
    from concourse.bass_utils import run_bass_kernel_spmd

    a = {k: np.asarray(x) for k, x in inputs.items()}

    def chunks(w):
        return w.T.reshape(-1, P, w.shape[0]).transpose(1, 0, 2)

    f = np.float32
    W = np.zeros((HK + 2, P, WG), f)
    W[0, :, W_BASE0:W_AR] = chunks(a["L0_cond_W"]).reshape(P, -1)
    ar = np.concatenate([a["L0_cond_A"].reshape(E * R0, DM), a["L0_cond_Wr"]], 0)
    W[0, :, W_AR:W_AR + KC * AR] = chunks(ar).reshape(P, -1)
    W[0, :, W_BASE1:] = chunks(a["L1_cond_W"]).reshape(P, -1)
    W[HK + 1, :, W_BASE3:] = chunks(a["L3_cond_W"]).reshape(P, -1)
    for g in range(HK):
        rows = slice(g * REP * D, (g + 1) * REP * D)
        kv = np.concatenate([a["L2_cond_Wk"][g * D:(g + 1) * D], a["L2_cond_Wv"][g * D:(g + 1) * D]], 0)
        W[g + 1, :, W_Q:W_KV] = chunks(a["L2_cond_Wq"][rows]).reshape(P, -1)
        W[g + 1, :, W_KV:W_O] = chunks(kv).reshape(P, -1)
        W[g + 1, :, W_O:] = a["L2_cond_Wo"][:, rows].T.reshape(REP, D, DM).transpose(1, 0, 2).reshape(P, -1)
    half_pow = (10000.0 ** (np.arange(0, D, 2) / D)).astype(f)
    arrays = {
        "x": np.ascontiguousarray(a["x"]),
        "xT": np.ascontiguousarray(a["x"].reshape(B, T, KC, P).transpose(3, 0, 2, 1)),
        "W": W,
        "a1": np.ascontiguousarray(a["L1_cond_lora_A"].reshape(-1, KC, P, R1).transpose(0, 2, 1, 3)),
        "b1": np.ascontiguousarray(a["L1_cond_lora_B_w"].T),
        "a3": np.ascontiguousarray(a["L3_cond_lora_As"].reshape(-1, KC, P, R3).transpose(0, 2, 1, 3)),
        "b3": np.ascontiguousarray(a["L3_cond_lora_Bs"]),
        "bcat0": np.ascontiguousarray(a["L0_cond_B"].transpose(0, 2, 1).reshape(E * R0, DM)),
        "bias3": np.ascontiguousarray(a["L3_cond_b"]),
        "kv_cache": np.concatenate([a["L2_cond_k_cache"], a["L2_cond_v_cache"]], -1).transpose(2, 0, 1, 3)
        .reshape(HK * PAGES * PSIZE, 2 * D),
        "table": np.ascontiguousarray(a["itok_Bx16_0_63"].reshape(B, KCT, P // PSIZE).transpose(2, 0, 1))
        .reshape(P // PSIZE, B * KCT),
        "q_w": np.ascontiguousarray(a["L2_cond_q_norm_w"]),
        "k_w": np.ascontiguousarray(a["L2_cond_k_norm_w"]),
        "inv_freq": f(1) / half_pow,
        "ids": np.concatenate([a["itok_B_0_2"], a["itok_B_0_23"],
                               a["itok_B_207_1644"], a["itok_B_0_7"]]),
    }
    nc = bacc.Bacc("TRN2", target_bir_lowering=False, num_devices=1)
    args = {k: nc.dram_tensor(f"in_{k}", x.shape, mybir.dt.from_np(x.dtype), kind="ExternalInput").ap()
            for k, x in arrays.items()}
    out = nc.dram_tensor("out_0", (B, T, DM), FP32, kind="ExternalOutput").ap()
    build(nc, out=out, **args)
    r = run_bass_kernel_spmd(nc, [{f"in_{k}": x for k, x in arrays.items()}], core_ids=[0])
    return r.results[0]["out_0"]
```

```python
from contextlib import ExitStack

import numpy as np

import concourse.bass as bass
from concourse import mybir

FP32 = mybir.dt.float32
FP32R = mybir.dt.float32r
BF16 = mybir.dt.bfloat16
I32 = mybir.dt.int32
U32 = mybir.dt.uint32
ALU = mybir.AluOpType
ACT = mybir.ActivationFunctionType

B, T, DM = 8, 128, 512
P = 128
KC = DM // P
E, R0 = 8, 16
R1, R3 = 32, 16
HQ, HK, D = 32, 8, 128
REP = HQ // HK
PAGES, PSIZE, NPP = 64, 32, 16
L = NPP * PSIZE
NK = L + T
KT = NK // P
KCT = L // P
N_IT = HK * B
EPS = 1e-6
LANG_BIAS, SCALING0, SCALING1, SCALING3 = 5.0, 2.0, 0.5, 2.0
MASKED = -1e30

WG = 5120
NPIECE = 8
WPIECE = WG // NPIECE
AR = E * R0 + E
W_Q, W_KV, W_O = 0, KC * REP * D, KC * (REP * D + 2 * D)
W_AR, W_BASE0, W_BASE1, W_BASE3 = 0, KC * AR, W_O, W_O

TWO_PI = 2 * np.pi
C1 = 6.28125
C2 = float(np.float32(int((TWO_PI - C1) * 2.0**21) / 2.0**21))
C3 = float(np.float32(TWO_PI - C1 - C2))
ROUND = float(1.5 * 2**23)
PI_BELOW = float(np.float32(3.1415925))


def ge(eng, sem, value):
    if isinstance(value, int) and value <= 0:
        return
    eng.wait_ge(sem, value)


def wait_apart(eng, sem, value, passed):
    eng.wait_ge(sem, value)
    if not isinstance(value, int):
        eng.sem_inc(passed, 1)


def matmul3(pe, out, lhs, rhs, start, stop):
    pe.matmul(out, lhs[0], rhs[0], start=start, stop=False)
    pe.matmul(out, lhs[0], rhs[1], start=False, stop=False)
    return pe.matmul(out, lhs[1], rhs[0], start=False, stop=stop)


def f32(ap):
    return ap.bitcast(FP32)


def build(nc, x, xT, W, a1, b1, a3, b3, bcat0, bias3, kv_cache, table, q_w, k_w, inv_freq, ids, out):
    ctx = ExitStack()
    with ctx:
        def sb(name, shape, dt=FP32):
            return ctx.enter_context(nc.sbuf_tensor(name, shape, dt))

        def sem(name):
            return ctx.enter_context(nc.semaphore(name))

        resid = sb("resid", [P, B, DM])
        xTr = sb("xTr", [P, B, KC, T])
        WH = sb("WH", [P, 2 * WG], FP32R)
        WL = sb("WL", [P, 2 * WG], FP32R)
        Wraw = sb("Wraw", [P, WPIECE])
        ident = sb("ident", [P, P])
        tabs = sb("tabs", [P, B, 4, D])
        mask_all = sb("mask_all", [P, B, L], BF16)
        mask = sb("mask", [P, NK], BF16)
        adapters = sb("adapters", [P, B * KC * R1])
        adapter_rows = sb("adapter_rows", [P, B + 1], U32)
        select = sb("select", [P, 2, B])
        chosen = sb("chosen", [P, 2])
        key_rows = sb("key_rows", [P, N_IT * KCT], U32)
        rows = sb("rows", [P, KCT], U32)
        biasb = sb("biasb", [P, DM])
        neg_half = sb("neg_half", [P, 8])
        lengths = sb("lengths", [P, B])
        XH = sb("XH", [P, KC, T], FP32R)
        XL = sb("XL", [P, KC, T], FP32R)
        KV = sb("KV", [P, KT, 2 * D])
        VH = sb("VH", [P, KT, D], FP32R)
        VL = sb("VL", [P, KT, D], FP32R)
        KTH = sb("KTH", [P, NK], FP32R)
        KTL = sb("KTL", [P, NK], FP32R)
        QTH = sb("QTH", [P, REP * T], FP32R)
        QTL = sb("QTL", [P, REP * T], FP32R)
        rt1 = sb("rt1", [P, (REP + 1) * D])
        rt2 = sb("rt2", [P, (REP + 1) * D])
        roped = sb("roped", [P, (REP + 1) * D])
        knew = sb("knew", [P, D])
        S = sb("S", [P, REP, NK])
        PH = sb("PH", [P, 3, REP * T], FP32R)
        PL = sb("PL", [P, 3, REP * T], FP32R)
        OH = sb("OH", [P, REP * T], FP32R)
        OL = sb("OL", [P, REP * T], FP32R)
        squares = sb("squares", [P, (REP + 1) * D], BF16)
        ssq = sb("ssq", [P, REP + 1])
        var = sb("var", [P, REP + 1])
        rstd = sb("rstd", [P, REP + 1])
        mx = sb("mx", [P, REP])
        nbias = sb("nbias", [P, REP])
        rsum = sb("rsum", [P, REP])
        rinv = sb("rinv", [P, REP])

        SP = [ctx.enter_context(nc.psum_tensor(f"SP{i}", [P, 1024], FP32)) for i in range(2)]
        PP = [ctx.enter_context(nc.psum_tensor(f"PP{i}", [P, 512], FP32)) for i in range(2)]
        MA = ctx.enter_context(nc.psum_tensor("MA", [P, 512], FP32))
        MB = ctx.enter_context(nc.psum_tensor("MB", [P, 512], FP32))

        passed = sem("passed")

        def piece_col(i):
            return ((i + 2 * NPIECE) % (2 * NPIECE)) * WPIECE

        def split(eng, hi, lo, src, hi_done, count):
            eng.tensor_scalar(hi, src, 1.0, 1.0, ALU.mult, ALU.mult).then_inc(hi_done, 1)
            wait_apart(eng, hi_done, count, passed)
            return eng.tensor_tensor(lo, src, f32(hi), ALU.subtract)

        def low_part(lo, hi, src):
            return nc.gpsimd.tensor_tensor(lo, src, f32(hi), ALU.subtract)

        adapters1_in, adapters3_in, ab_high, ab_split = (
            sem(n) for n in ("adapters1_in", "adapters3_in", "ab_high", "ab_split"))
        x_high, x_split, rows_copied, kv_loaded = (
            sem(f"a_{n}") for n in ("x_high", "x_split", "rows_copied", "kv_loaded"))
        layer0(nc, sem, locals())
        lora_layer(nc, sem, locals(), "l1", 0, R1, W_BASE1 + WG, None)
        attention(nc, sem, locals())
        lora_layer(nc, sem, locals(), "l3", 1, R3, W_BASE3, out)


def layer0(nc, sem, v):
    ident, tabs, mask, neg_half, WH, WL, Wraw, resid, xTr, XH, XL, KV, S, select = (v[k] for k in (
        "ident tabs mask neg_half WH WL Wraw resid xTr XH XL KV S select").split())
    SP, PP, MT, rt1, rt2, roped, knew = v["SP"], v["PP"], (v["MA"], v["MB"]), v["rt1"], v["rt2"], v["roped"], v["knew"]
    NH = E * R0
    flat_tabs = tabs[:, :, :, :].rearrange("p b n d -> p (b n d)")
    third = (KC * AR + KC * DM) // 2
    ends = [0, third, 2 * third, 3 * third, 3 * third + WPIECE, WG]
    part_raw = [flat_tabs[:, 0:third], flat_tabs[:, third:2 * third], flat_tabs[:, 2 * third:3 * third], Wraw[:, :],
                v["adapters"][:, 0:ends[5] - ends[4]]]
    w = WG
    part_hi_lo = [(WH[:, w + ends[i]:w + ends[i + 1]], WL[:, w + ends[i]:w + ends[i + 1]]) for i in range(5)]

    def pairs(t):
        return t.rearrange("p (b f) -> p b f", b=B)

    N2 = B * D // 2
    ang, turns, red, cosv = (pairs(S[:, i, 0:N2]) for i in range(4))
    Braw = S[:, :, N2:N2 + P]
    sinv, redc = pairs(rt2[:, 0:N2]), pairs(roped[:, 0:N2])
    keyno = rt1[:, 0:L]
    invf = knew[:, 0:D // 2]
    qw, kw = rt1[:, 512:640], KV[:, 0, 0:D]
    ids_i, ids_f = KV[:, 1, 0:4 * B].bitcast(I32), KV[:, 1, 32:32 + 4 * B]
    adapter_f, seqf, lang = ids_f[:, 0:2 * B], ids_f[:, 2 * B:3 * B], ids_f[:, 3 * B:4 * B]
    picked, slot, b_row, batch_in_side, batch_no = (
        KV[:, 1, 64 + 16 * i:64 + 16 * i + n] for i, n in enumerate((B, 2, 1, B, B)))
    pos, tokno, key_in_page = (KV[:, 2, 16 * i:16 * i + B] for i in range(3))
    pages_i = KV[:, 3, 0:B * KCT].bitcast(I32)
    pages, first_rows = (KV[:, 4, 32 * i:32 * i + B * KCT] for i in range(2))
    enum, lang_bias = rt2[:, 512:512 + B * E], roped[:, 512:512 + B * E]
    all8 = lambda t: t.rearrange("p (b e) -> p b e", b=B)
    small = [[KV[:, 0, 128 + 64 * u + 8 * i:136 + 64 * u + 8 * i] for i in range(8)] for u in range(2)]
    diff, ediff, esum, w0, w1 = ([KV[:, 2, 128 + 8 * u + i:129 + 8 * u + i] for u in range(2)] for i in range(5))
    hg = [KV[:, 3 + u, 128:128 + NH] for u in range(2)]
    X = [[t[:, :, :].rearrange("p c t -> p (c t)") for t in (XH, XL)], [v[t][:, 0:DM] for t in ("KTH", "KTL")]]
    H = [(v["OH"][:, u * NH:(u + 1) * NH], v["OL"][:, u * NH:(u + 1) * NH]) for u in range(2)]
    BH, BL = v["PH"][:, 0, :], v["PL"][:, 0, :]
    names = ("const ids_in invf_in norms_in x0T_in xT_in x_in pages_in pages_done b_in zeros part_high part_split "
             "rest_split b1_in b_high b_split trig angles sines misc x_high x_split routed base logits top place "
             "diff exp index w0 w1 g gated hT hT_high hT_split lora added").split()
    (const, ids_in, invf_in, norms_in, x0T_in, xT_in, x_in, pages_in, pages_done, b_in, zeros, part_high, part_split,
     rest_split, b1_in, b_high, b_split, trig, angles, sines, misc, x_high, x_split, routed, base_done, logits_done,
     top_done, place_done, diff_done, exp_done, index_done, w0_done, w1_done, g_done, gated, hT_done, hT_high,
     hT_split, lora_done, added) = (
         sem(f"l0_{n}") for n in names)
    part_in = [sem(f"l0_part{i}_in") for i in range(5)]
    N_CONST = 5 + P // PSIZE
    exists = step_exists

    def batch(t, b):
        return t[:, bass.ds(b, 1), :].rearrange("p a d -> p (a d)")

    def batch_xT(b):
        return xTr[:, bass.ds(b, 1), :, :].rearrange("p a c t -> p (a c t)")

    with nc.Block() as block:
        @block.sync
        def _(sp):
            sp.dma_start(ids_i, v["ids"].partition_broadcast(P)).then_inc(ids_in, 16)
            for i in range(5):
                sp.dma_start(part_raw[i], v["W"][0, :, ends[i]:ends[i + 1]]).then_inc(part_in[i], 16)
                if i == 1:
                    sp.dma_start(Braw, v["bcat0"].rearrange("k (a n) -> k a n", a=REP)).then_inc(b_in, 16)
            for q in range(P // PSIZE):
                sp.dma_start(pages_i[q * PSIZE:(q + 1) * PSIZE, :], v["table"][q, :].partition_broadcast(PSIZE))\
                    .then_inc(pages_in, 16)
            sp.wait_ge(rest_split, 2)
            for q in range(P // R1):
                sp.dma_start(Wraw[q * R1:(q + 1) * R1, 0:DM], v["b1"]).then_inc(b1_in, 16)
            sp.wait_ge(rest_split, 3)
            sp.wait_ge(ids_in, 16)
            with sp.Fori(0, B) as b:
                a = sp.value_load(ids_i[0:1, bass.ds(b, 1)], min_val=0, max_val=v["a1"].shape[0] - 1)
                sp.dma_start(v["adapters"][:, bass.ds(b * KC * R1, KC * R1)],
                             v["a1"][bass.ds(a, 1), :, :].rearrange("a p n -> p (a n)")).then_inc(v["adapters1_in"], 16)

        @block.scalar
        def _(act):
            def high_x(k, u, b):
                ge(act, base_done, k - 1)
                act.activation(X[u][0], batch_xT(b), ACT.Copy).then_inc(x_high, 1)

            def high_part(i):
                act.wait_ge(part_in[i], 16)
                act.activation(part_hi_lo[i][0], part_raw[i], ACT.Copy).then_inc(part_high, 1)

            def high_h(k, u):
                act.wait_ge(hT_done, k + 1)
                ge(act, lora_done, k - 1)
                act.activation(H[u][0], MT[u][:, 0:NH], ACT.Copy).then_inc(hT_high, 1)

            def step(k, u, b):
                if past_first(k) and exists(k + 1):
                    high_x(k + 1, 1 - u, batch_after(u, b))
                if exists(k - 1):
                    high_h(k - 1, 1 - u)
                act.wait_ge(diff_done, k + 1)
                act.activation(ediff[u], diff[u], ACT.Exp).then_inc(exp_done, 1)
                if not past_first(k):
                    act.wait_ge(angles, 1)
                    act.activation(sinv, red, ACT.Sin).then_inc(sines, 1)
                    act.activation(cosv, redc, ACT.Sin).then_inc(sines, 1)

            act.dma_start(invf, v["inv_freq"].partition_broadcast(P)).then_inc(invf_in, 16)
            act.dma_start(xTr[:, 0, :, :], v["xT"][:, 0, :, :]).then_inc(x0T_in, 16)
            act.dma_start(xTr[:, 1:B, :, :], v["xT"][:, 1:B, :, :]).then_inc(xT_in, 16)
            act.wait_ge(x0T_in, 16)
            high_x(0, 0, 0)
            high_part(0)
            high_part(1)
            act.dma_start(resid[:, :, :], v["x"].rearrange("b t d -> t b d")).then_inc(x_in, 16)
            for dst, src in ((qw, v["q_w"]), (kw, v["k_w"]), (v["biasb"][:, :], v["bias3"])):
                act.dma_start(dst, src.partition_broadcast(P)).then_inc(norms_in, 16)
            act.wait_ge(xT_in, 16)
            high_x(1, 1, B // 2)
            act.wait_ge(b_in, 16)
            act.activation(BH.rearrange("p (a n) -> p a n", a=REP), Braw, ACT.Copy).then_inc(b_high, 1)
            for i in range(2, 5):
                high_part(i)
            over_batches(act, step)
            high_h(B - 1, 1)
            act.wait_ge(norms_in, 48)

        @block.gpsimd
        def _(pool):
            def iota(out, pattern, per_partition):
                pool.iota(out, pattern=pattern, base=0, channel_multiplier=per_partition,
                          allow_small_or_imprecise_dtypes=True).then_inc(const, 1)

            iota(tokno[:, 0:1], [[0, 1]], 1)
            iota(enum, [[0, B], [1, E]], 0)
            iota(batch_no, [[1, B]], 0)
            iota(batch_in_side, [[0, B * R1 // P], [1, P // R1]], 0)
            iota(keyno, [[1, L]], 0)
            for q in range(P // PSIZE):
                pool.wait_ge(const, 5 + q)
                iota(key_in_page[q * PSIZE:(q + 1) * PSIZE, 0:1], [[0, 1]], 1)
            pool.wait_ge(const, N_CONST)
            pool.memset(ident[:, :], 0.0).then_inc(zeros, 1)
            pool.wait_ge(zeros, 1)
            pool.affine_select(out=ident[:, :], in_=ident[:, :], compare_op=ALU.not_equal, fill=1.0, base=0,
                               pattern=[[-1, P]], channel_multiplier=1).then_inc(zeros, 1)
            pool.memset(neg_half[:, :], -0.5)
            pool.memset(mask[:, :], 0.0)
            for i in range(2, 5):
                wait_apart(pool, part_high, i + 1, v["passed"])
                v["low_part"](part_hi_lo[i][1], part_hi_lo[i][0], part_raw[i]).then_inc(rest_split, 1)
            pool.wait_ge(norms_in, 48)
            pool.wait_ge(sines, 2)
            pool.wait_ge(rest_split, 3)
            full = [P, B, 2, D // 2]
            for n, (t, norm) in enumerate(((cosv, qw), (sinv, qw), (cosv, kw), (sinv, kw))):
                pool.tensor_tensor(tabs[:, :, n, :].rearrange("p b (a f) -> p b a f", a=2),
                                   t.unsqueeze(2).broadcast_to(full),
                                   norm.rearrange("p (a f) -> p a f", a=2).unsqueeze(1).broadcast_to(full), ALU.mult)
            pool.wait_ge(pages_in, 16 * P // PSIZE)
            pool.tensor_copy(pages, pages_i).then_inc(pages_done, 1)
            pool.wait_ge(pages_done, 1)
            pool.tensor_scalar(first_rows, pages, float(PSIZE), key_in_page[:, 0:1], ALU.mult, ALU.add)\
                .then_inc(pages_done, 1)
            pool.wait_ge(pages_done, 2)
            for g in range(HK):
                pool.tensor_scalar(v["key_rows"][:, g * B * KCT:(g + 1) * B * KCT], first_rows, 1.0,
                                   float(g * PAGES * PSIZE), ALU.mult, ALU.add)
            pool.wait_ge(b1_in, 16 * P // R1)
            split_adapters(pool, v, 0, R1, Wraw[:, 0:DM], v["adapters1_in"])

        @block.vector
        def _(dve):
            count = {trig: 0, misc: 0}

            def done(ins, chain):
                count[chain] += 1
                ins.then_inc(chain, 1)
                dve.wait_ge(chain, count[chain])

            def find_angles():
                half = [P, B, D // 2]
                dve.wait_ge(ids_in, 16)
                dve.wait_ge(const, N_CONST)
                done(dve.tensor_copy(ids_f, ids_i), trig)
                done(dve.tensor_scalar(pos, seqf, tokno[:, 0:1], None, ALU.add), trig)
                dve.tensor_copy(v["lengths"][:, :], seqf)
                dve.wait_ge(invf_in, 16)
                done(dve.tensor_tensor(ang, pos.unsqueeze(2).broadcast_to(half),
                                       invf.unsqueeze(1).broadcast_to(half), ALU.mult), trig)
                done(dve.tensor_scalar(turns, ang, float(1 / TWO_PI), ROUND, ALU.mult, ALU.add), trig)
                done(dve.tensor_scalar(turns, turns, ROUND, None, ALU.subtract), trig)

            def reduce_angles():
                done(dve.scalar_tensor_tensor(out=red, in0=turns, scalar=-C1, in1=ang, op0=ALU.mult, op1=ALU.add), trig)
                done(dve.scalar_tensor_tensor(out=ang, in0=turns, scalar=-C2, in1=red, op0=ALU.mult, op1=ALU.add), trig)
                done(dve.scalar_tensor_tensor(out=red, in0=turns, scalar=-C3, in1=ang, op0=ALU.mult, op1=ALU.add), trig)
                done(dve.tensor_scalar(redc, red, float(np.pi / 2), None, ALU.add), trig)
                done(dve.tensor_scalar(turns, redc, PI_BELOW, -TWO_PI, ALU.is_gt, ALU.mult), trig)
                done(dve.tensor_tensor(redc, redc, turns, ALU.add), trig)
                dve.tensor_scalar(red, red, PI_BELOW, -PI_BELOW, ALU.min, ALU.max)
                dve.tensor_scalar(redc, redc, PI_BELOW, -PI_BELOW, ALU.min, ALU.max).then_inc(angles, 1)

            def find_rows():
                for i, r in enumerate((R1, R3)):
                    last = dve.tensor_scalar(slot[:, i:i + 1], tokno[:, 0:1], 1.0 / r, -(r - 1) / (2 * r),
                                             ALU.mult, ALU.add)
                done(last, misc)
                done(dve.tensor_scalar(slot, slot, ROUND, None, ALU.add), misc)
                done(dve.tensor_scalar(slot, slot, ROUND, None, ALU.subtract), misc)
                dve.tensor_scalar(select[:, 0, :], batch_in_side, slot[:, 0:1], SCALING1, ALU.is_equal, ALU.mult)
                done(dve.tensor_scalar(select[:, 1, :], batch_no, slot[:, 1:2], None, ALU.is_equal), misc)
                done(dve.tensor_tensor_reduce(out=picked, in0=select[:, 1, :], in1=adapter_f[:, B:2 * B], scale=1.0,
                                              scalar=0.0, op0=ALU.mult, op1=ALU.add, accum_out=b_row), misc)
                dve.tensor_scalar(select[:, 1, :], select[:, 1, :], SCALING3, None, ALU.mult)
                done(dve.tensor_scalar(b_row, b_row, slot[:, 1:2], None, ALU.subtract), misc)
                dve.tensor_scalar(v["adapter_rows"][:, B:B + 1], b_row, float(R3), tokno[:, 0:1],
                                  ALU.mult, ALU.add)
                dve.tensor_scalar(v["adapter_rows"][:, 0:B], adapter_f[:, B:2 * B], float(P), tokno[:, 0:1],
                                  ALU.mult, ALU.add)

            def low_part_of(i):
                dve.wait_ge(part_high, i + 1)
                dve.tensor_tensor(part_hi_lo[i][1], part_raw[i], f32(part_hi_lo[i][0]), ALU.subtract)\
                    .then_inc(part_split, 1)

            def low_x(k, u, b):
                dve.wait_ge(x_high, k + 1)
                dve.tensor_tensor(X[u][1], batch_xT(b), f32(X[u][0]), ALU.subtract).then_inc(x_split, 1)

            def choose(k, u, b):
                logit, top, place, place_f = (small[u][i] for i in range(4))
                dve.wait_ge(routed, k + 1)
                dve.tensor_tensor(logit, PP[u][:, NH:AR], lang_bias[:, bass.ds(b * E, E)], ALU.add)\
                    .then_inc(logits_done, 1)
                wait_apart(dve, logits_done, k + 1, v["passed"])
                dve.max(top, logit).then_inc(top_done, 1)
                dve.wait_ge(top_done, k + 1)
                dve.tensor_tensor(diff[u], top[:, 1:2], top[:, 0:1], ALU.subtract).then_inc(diff_done, 1)
                wait_apart(dve, diff_done, k + 1, v["passed"])
                dve.max_index(place.bitcast(U32), top, logit).then_inc(place_done, 1)
                dve.wait_ge(place_done, k + 1)
                dve.tensor_copy(place_f, place.bitcast(U32)).then_inc(index_done, 1)

            def gate(k, u):
                place_f, g0, g1 = (small[u][i] for i in (3, 4, 5))
                dve.wait_ge(exp_done, k + 1)
                dve.tensor_scalar(esum[u], ediff[u], 1.0, None, ALU.add).then_inc(w0_done, 1)
                dve.wait_ge(w0_done, 2 * k + 1)
                dve.reciprocal(w0[u], esum[u]).then_inc(w0_done, 1)
                dve.wait_ge(index_done, k + 1)
                dve.wait_ge(w0_done, 2 * k + 2)
                dve.tensor_tensor(w1[u], w0[u], ediff[u], ALU.mult).then_inc(w1_done, 1)
                dve.tensor_scalar(g0, enum[:, 0:E], place_f[:, 0:1], w0[u], ALU.is_equal, ALU.mult)
                dve.wait_ge(w1_done, k + 1)
                dve.tensor_scalar(g1, enum[:, 0:E], place_f[:, 1:2], w1[u], ALU.is_equal, ALU.mult).then_inc(g_done, 1)
                dve.wait_ge(g_done, 2 * k + 1)
                dve.tensor_tensor(g0, g0, g1, ALU.add).then_inc(g_done, 1)
                dve.wait_ge(g_done, 2 * k + 2)
                ge(dve, hT_done, k - 1)
                dve.scalar_tensor_tensor(out=hg[u].rearrange("p (e r) -> p e r", e=E),
                                         in0=PP[u][:, 0:NH].rearrange("p (e r) -> p e r", e=E), scalar=SCALING0,
                                         in1=g0.unsqueeze(2).broadcast_to([P, E, R0]), op0=ALU.mult,
                                         op1=ALU.mult).then_inc(gated, 1)

            def low_h(k, u):
                dve.wait_ge(hT_high, k + 1)
                dve.tensor_tensor(H[u][1], MT[u][:, 0:NH], f32(H[u][0]), ALU.subtract).then_inc(hT_split, 1)

            def add(k, u, b):
                dve.wait_ge(lora_done, k + 1)
                dve.tensor_tensor(batch(resid, b), SP[u][:, 0:DM], batch(resid, b), ALU.add).then_inc(added, 1)

            def step(k, u, b):
                choose(k, u, b)
                if exists(k - 1):
                    low_h(k - 1, 1 - u)
                if past_first(k) and exists(k + 1):
                    low_x(k + 1, 1 - u, batch_after(u, b))
                gate(k, u)
                if exists(k - 1):
                    if isinstance(k, int) and k == B - 1:
                        find_rows()
                    if isinstance(k, int) and k == 1:
                        dve.wait_ge(x_in, 16)
                    add(k - 1, 1 - u, batch_before(u, b))

            find_angles()
            low_x(0, 0, 0)
            low_part_of(0)
            low_part_of(1)
            reduce_angles()
            low_x(1, 1, B // 2)
            dve.wait_ge(b_high, 1)
            dve.tensor_tensor(BL.rearrange("p (a n) -> p a n", a=REP), Braw,
                              f32(BH).rearrange("p (a n) -> p a n", a=REP), ALU.subtract).then_inc(b_split, 1)
            done(dve.tensor_tensor(all8(lang_bias), all8(enum), lang.unsqueeze(2).broadcast_to([P, B, E]),
                                   ALU.is_equal), misc)
            done(dve.tensor_scalar(lang_bias, lang_bias, LANG_BIAS, None, ALU.mult), misc)
            over_batches(dve, step)
            low_h(B - 1, 1)
            add(B - 1, 1, B - 1)

        @block.tensor
        def _(pe):
            def x_of(u, c):
                return X[u][0][:, c * T:(c + 1) * T], X[u][1][:, c * T:(c + 1) * T]

            def route(k, u):
                pe.wait_ge(x_split, k + 1)
                ge(pe, gated, k - 1)
                for c in range(KC):
                    at = w + W_AR + c * AR
                    last = matmul3(pe, PP[u][:, 0:AR], x_of(u, c), (WH[:, at:at + AR], WL[:, at:at + AR]), c == 0,
                                   c == KC - 1)
                last.then_inc(routed, 1)

            def times_w(k, u, chunks):
                if chunks[0] == 0:
                    ge(pe, added, k - 1)
                for c in chunks:
                    at = w + W_BASE0 + c * DM
                    last = matmul3(pe, SP[u][:, 0:DM], x_of(u, c), (WH[:, at:at + DM], WL[:, at:at + DM]), c == 0,
                                   False)
                if chunks[-1] == KC - 1:
                    last.then_inc(base_done, 1)

            def transpose_h(k, u):
                pe.wait_ge(gated, k + 1)
                ge(pe, hT_split, k - 1)
                if isinstance(k, int) and k == 0:
                    pe.wait_ge(zeros, 2)
                pe.transpose(MT[u][:, 0:NH], hg[u], ident[:, :]).then_inc(hT_done, 1)

            def times_b(k, u):
                pe.wait_ge(hT_split, k + 1)
                if isinstance(k, int) and k == 0:
                    pe.wait_ge(b_split, 1)
                matmul3(pe, SP[u][:, 0:DM], H[u], (BH, BL), False, True).then_inc(lora_done, 1)

            def step(k, u, b):
                if isinstance(k, int) and k == 0:
                    pe.wait_ge(part_split, 1)
                route(k, u)
                if isinstance(k, int) and k == 0:
                    pe.wait_ge(part_split, 2)
                if exists(k - 1):
                    transpose_h(k - 1, 1 - u)
                times_w(k, u, range(KC - 1))
                if exists(k - 1):
                    times_b(k - 1, 1 - u)
                times_w(k, u, range(KC - 1, KC))

            over_batches(pe, step)
            transpose_h(B - 1, 1)
            times_b(B - 1, 1)


def load_last_adapters(pool, v):
    n = KC * R3
    for b in range(B):
        pool.indirect_dma_start(v["adapters"][:, b * n:(b + 1) * n], None, v["a3"], bass.IndirectOffsetOnAxis(
            ap=v["adapter_rows"][:, b:b + 1], axis=0)).then_inc(v["adapters3_in"], 16)
    pool.indirect_dma_start(v["adapters"][:, B * n:B * n + DM], None, v["b3"], bass.IndirectOffsetOnAxis(
        ap=v["adapter_rows"][:, B:B + 1], axis=0)).then_inc(v["adapters3_in"], 16)


def adapter_parts(v, rank):
    flat = lambda t: v[t][:, :, :].rearrange("p a b -> p (a b)")[:, 0:KC * P]
    A = [(v["QTH"][:, :], v["QTL"][:, :]), (flat("VH"), flat("VL"))][0:B * rank // P]
    return A, (v["PH"][:, 1, :], v["PL"][:, 1, :])


def split_adapters(pool, v, layer, rank, Braw, loaded, a_free=None, b_free=None):
    A, B_parts = adapter_parts(v, rank)
    done = layer * (B * R1 // P + 1)
    pool.wait_ge(loaded, 16 * (B + layer))
    if a_free:
        pool.wait_ge(*a_free)
    for g, pair in enumerate(A):
        raw = v["adapters"][:, g * KC * P:(g + 1) * KC * P].rearrange("p (b c r) -> p c b r", b=P // rank, c=KC)
        hi, lo = (t.rearrange("p (c b r) -> p c b r", c=KC, b=P // rank) for t in pair)
        done += 1
        v["split"](pool, hi, lo, raw, v["ab_high"], done).then_inc(v["ab_split"], 1)
    if b_free:
        pool.wait_ge(*b_free)
    v["split"](pool, *B_parts, Braw, v["ab_high"], done + 1).then_inc(v["ab_split"], 1)


def gather(pool, v, j):
    pool.tensor_copy(v["rows"][:, :], v["key_rows"][:, bass.ds(j * KCT, KCT)]).then_inc(v["rows_copied"], 1)
    wait_apart(pool, v["rows_copied"], j + 1, v["passed"])
    for t in range(KCT):
        pool.indirect_dma_start(v["KV"][:, t, :], None, v["kv_cache"],
                                bass.IndirectOffsetOnAxis(ap=v["rows"][:, t:t + 1], axis=0))\
            .then_inc(v["kv_loaded"], 16)


def over_batches(eng, body):
    half = B // 2
    body(0, 0, 0)
    body(1, 1, half)
    with eng.Fori(1, half - 1) as m:
        body(2 * m, 0, m)
        body(2 * m + 1, 1, m + half)
    body(B - 2, 0, half - 1)
    body(B - 1, 1, B - 1)


def step_exists(k):
    return not isinstance(k, int) or 0 <= k < B


def past_first(k):
    return not isinstance(k, int) or k > 0


def batch_after(u, b):
    return b + B // 2 if u == 0 else b - B // 2 + 1


def batch_before(u, b):
    return b + B // 2 - 1 if u == 0 else b - B // 2


def lora_layer(nc, sem, v, name, layer, rank, wbase, out):
    resid, xTr, XH, XL, WH, WL, ident, chosen = (
        v[k] for k in ("resid", "xTr", "XH", "XL", "WH", "WL", "ident", "chosen"))
    SP, PP, MT = v["SP"], v["PP"], (v["MA"], v["MB"])
    kv = v["KV"][:, :, :].rearrange("p a b -> p (a b)")
    S = v["S"]
    select = v["select"][:, layer, :]
    hi_lo, (BH, BL) = adapter_parts(v, rank)
    groups = len(hi_lo)
    A = [[t.rearrange("p (c r) -> p c r", c=KC) for t in pair] for pair in hi_lo]
    X = [[t[:, :, :].rearrange("p c t -> p (c t)") for t in (XH, XL)], [v[t][:, 0:DM] for t in ("KTH", "KTL")]]
    xs = [S[:, u, 0:DM] for u in range(2)]
    y = [S[:, 2 + u, 0:DM] for u in range(2)]
    xo = [kv[:, u * DM:(u + 1) * DM] for u in range(2)]
    low = [(v["OH"][:, u * T:(u + 1) * T], v["OL"][:, u * T:(u + 1) * T]) for u in range(2)]
    names = ("x_copied", "x_biased", "xT", "xT_high", "xT_split", "low", "chosen",
             "low_high", "low_split", "base", "y", "yT", "yT_kept", "y_kept", "stored0", "stored1",
             "w_loaded0", "w_loaded1", "w_high", "w_split")
    (x_copied, x_biased, xT_done, xT_high, xT_split, low_done, chosen_done,
     low_high, low_split, base_done, y_done, yT_done, yT_kept, y_kept, stored0, stored1, w_loaded0,
     w_loaded1, w_high, w_split) = (sem(f"{name}_{m}") for m in names)
    stored, w_loaded = (stored0, stored1), (w_loaded0, w_loaded1)
    Wraw = v["Wraw"][:, :], v["rt2"][:, 0:WPIECE]
    last_layer = out is not None
    exists = step_exists

    def row(b):
        return resid[:, bass.ds(b, 1), :].rearrange("p a d -> p (a d)")

    with nc.Block() as block:
        @block.sync
        def _(sp):
            def load_piece(k, u, b):
                ge(sp, w_split, k - 1)
                sp.dma_start(Wraw[u], v["W"][1, :, bass.ds(k * WPIECE, WPIECE)]).then_inc(w_loaded[u], 16)

            def store(k, u, b):
                sp.wait_ge(y_done, k + 1)
                sp.dma_start(out[bass.ds(b, 1), :, :].rearrange("a t d -> (a t) d"), y[u])\
                    .then_inc(stored[u], 16)

            if last_layer:
                over_batches(sp, store)
                for u in range(2):
                    sp.wait_ge(stored[u], 16 * B // 2)
            else:
                over_batches(sp, load_piece)

        @block.gpsimd
        def _(pool):
            def split_piece(k, u, b):
                wait_apart(pool, w_high, k + 1, v["passed"])
                at = bass.ds(k * WPIECE, WPIECE)
                v["low_part"](WL[:, at], WH[:, at], Wraw[u]).then_inc(w_split, 1)

            def add_bias(k, u, b):
                if exists(k - 2):
                    wait_apart(pool, y_done, k - 1, v["passed"])
                pool.tensor_tensor(xo[u], row(b), v["biasb"][:, :], ALU.add).then_inc(x_biased, 1)

            if last_layer:
                over_batches(pool, add_bias)
            else:
                gather(pool, v, 0)
                load_last_adapters(pool, v)
                over_batches(pool, split_piece)

        @block.scalar
        def _(act):
            def copy_x(k, u, b):
                if exists(k - 2):
                    ge(act, xT_done, k - 1)
                    ge(act, y_done, k - 1)
                act.activation(xs[u], row(b), ACT.Copy).then_inc(x_copied, 1)

            def high_xT(k, u):
                act.wait_ge(xT_done, k + 1)
                ge(act, base_done, k - 1)
                act.activation(X[u][0], MT[u][:, :], ACT.Copy).then_inc(xT_high, 1)

            def high_low(k, u):
                act.wait_ge(chosen_done, k + 1)
                act.wait_ge(low_done, k + 1)
                ge(act, base_done, k - 1)
                act.activation(low[u][0], PP[u][:, 0:T], ACT.Copy, scale=chosen[:, u:u + 1]).then_inc(low_high, 1)

            def keep_y(k, u, b):
                act.wait_ge(y_done, k + 1)
                act.activation(row(b), y[u], ACT.Copy).then_inc(y_kept, 1)
                act.wait_ge(yT_done, k + 1)
                act.activation(xTr[:, bass.ds(b, 1), :, :].rearrange("p a c t -> p (a c t)"), SP[u][:, DM:2 * DM],
                               ACT.Copy).then_inc(yT_kept, 1)

            def step(k, u, b):
                high_low(k, u)
                if exists(k + 1):
                    high_xT(k + 1, 1 - u)
                if not last_layer and exists(k - 1):
                    keep_y(k - 1, 1 - u, batch_before(u, b))
                if exists(k + 2):
                    copy_x(k + 2, u, b + 1)
                if not last_layer:
                    act.wait_ge(w_loaded[u], 16 * (k // 2) + 16)
                    act.activation(WH[:, bass.ds(k * WPIECE, WPIECE)], Wraw[u], ACT.Copy).then_inc(w_high, 1)

            copy_x(0, 0, 0)
            copy_x(1, 1, B // 2)
            high_xT(0, 0)
            over_batches(act, step)
            if not last_layer:
                keep_y(B - 1, 1, B - 1)

        @block.vector
        def _(dve):
            def choose(k, u, b):
                dve.tensor_copy(chosen[:, u:u + 1], select[:, bass.ds(b, 1)]).then_inc(chosen_done, 1)

            def low_xT(k, u):
                dve.wait_ge(xT_high, k + 1)
                dve.tensor_tensor(X[u][1], MT[u][:, :], f32(X[u][0]), ALU.subtract).then_inc(xT_split, 1)

            def low_low(k, u):
                dve.wait_ge(low_high, k + 1)
                dve.scalar_tensor_tensor(out=low[u][1], in0=PP[u][:, 0:T], scalar=chosen[:, u:u + 1],
                                         in1=f32(low[u][0]), op0=ALU.mult, op1=ALU.subtract).then_inc(low_split, 1)

            def add(k, u):
                dve.wait_ge(base_done, k + 1)
                if last_layer:
                    dve.wait_ge(x_biased, k + 1)
                    ge(dve, stored[u], 16 * (k // 2))
                else:
                    ge(dve, y_kept, k - 1)
                    ge(dve, yT_done, k - 1)
                    dve.wait_ge(x_copied, k + 1)
                dve.tensor_tensor(y[u], SP[u][:, 0:DM], xo[u] if last_layer else xs[u], ALU.add).then_inc(y_done, 1)

            def step(k, u, b):
                low_low(k, u)
                if exists(k + 1):
                    choose(k + 1, 1 - u, batch_after(u, b))
                    low_xT(k + 1, 1 - u)
                add(k, u)

            choose(0, 0, 0)
            low_xT(0, 0)
            if not last_layer:
                for b in range(B):
                    dve.tensor_scalar(v["mask_all"][:, b, :], v["rt1"][:, 0:L], v["lengths"][:, b:b + 1],
                                      MASKED, ALU.is_ge, ALU.mult)
            over_batches(dve, step)
            if not last_layer:
                dve.wait_ge(base_done, B - 1)
                dve.wait_ge(yT_kept, 1)
                dve.tensor_copy(X[0][0], xTr[:, 0, :, :].rearrange("p c t -> p (c t)")).then_inc(v["x_high"], 1)
                dve.wait_ge(v["x_high"], 1)
                dve.tensor_tensor(X[0][1], xTr[:, 0, :, :].rearrange("p c t -> p (c t)"), f32(X[0][0]), ALU.subtract)\
                    .then_inc(v["x_split"], 1)

        @block.tensor
        def _(pe):
            def transpose_x(k, u):
                pe.wait_ge(x_copied, k + 1)
                ge(pe, xT_split, k - 1)
                for c in range(KC):
                    last = pe.transpose(MT[u][:, c * T:(c + 1) * T], xs[u][:, c * P:(c + 1) * P], ident[:, :])
                last.then_inc(xT_done, 1)

            def transpose_y(k, u):
                pe.wait_ge(y_done, k + 1)
                ge(pe, yT_kept, k - 1)
                for c in range(KC):
                    last = pe.transpose(SP[u][:, DM + c * T:DM + (c + 1) * T], y[u][:, c * P:(c + 1) * P], ident[:, :])
                last.then_inc(yT_done, 1)

            def x_of(u, c):
                return X[u][0][:, c * T:(c + 1) * T], X[u][1][:, c * T:(c + 1) * T]

            def times_a(k, u):
                pe.wait_ge(xT_split, k + 1)
                ge(pe, low_split, k - 1)
                for c in range(KC):
                    last = matmul3(pe, PP[u][:, 0:T], [t[:, c, :] for t in A[u % groups]], x_of(u, c), c == 0,
                                   c == KC - 1)
                last.then_inc(low_done, 1)

            def times_w(k, u, chunks):
                if chunks[0] == 0:
                    ge(pe, y_done, k - 1)
                for c in chunks:
                    at = wbase + c * DM
                    matmul3(pe, SP[u][:, 0:DM], x_of(u, c), (WH[:, at:at + DM], WL[:, at:at + DM]), c == 0, False)

            def times_b(k, u):
                pe.wait_ge(low_split, k + 1)
                matmul3(pe, SP[u][:, 0:DM], low[u], (BH, BL), False, True).then_inc(base_done, 1)

            def step(k, u, b):
                times_a(k, u)
                times_w(k, u, range(KC // 2))
                if exists(k + 1):
                    transpose_x(k + 1, 1 - u)
                times_w(k, u, range(KC // 2, KC))
                if not last_layer and exists(k - 1):
                    transpose_y(k - 1, 1 - u)
                times_b(k, u)

            transpose_x(0, 0)
            over_batches(pe, step)
            if not last_layer:
                transpose_y(B - 1, 1)


def attention(nc, sem, v):
    (resid, xTr, XH, XL, WH, WL, Wraw, ident, tabs, mask_all, mask, KV, VH, VL, KTH, KTL, QTH, QTL, rt1, rt2, roped,
     knew, S, PH, PL, OH, OL, squares, ssq, var, rstd, mx, nbias, rsum, rinv, SP, PP, MA, MB,
     neg_half) = (v[k] for k in (
         "resid xTr XH XL WH WL Wraw ident tabs mask_all mask KV VH VL KTH KTL QTH QTL rt1 rt2 "
         "roped knew S PH PL OH OL squares ssq var rstd mx nbias rsum rinv SP PP MA MB neg_half").split())
    W = v["W"]
    names = ("mask_loaded w_loaded w_high w_split v_high v_split q_proj kv_proj "
             "kT kT_high kT_split q_stats q_mults q_roped q_var rstd_done kv_read k_mults k_roped k_var k_ready "
             "qT qT_high qT_split knT knT_high knT_split scores masked nbias exps rinv probs pT p_high p_split pv "
             "o_high o_split o_proj o_added").split()
    s = dict(zip(names, (sem(f"a_{n}") for n in names)))
    x_high, x_split, kv_loaded = v["x_high"], v["x_split"], v["kv_loaded"]
    (mask_loaded, w_loaded, w_high, w_split, v_high, v_split, q_proj, kv_proj,
     kT_done, kT_high, kT_split, q_stats, q_mults, q_roped, q_var, rstd_done, kv_read, k_mults, k_roped, k_var,
     k_ready, qT_done, qT_high, qT_split, knT_done, knT_high, knT_split, scored, masked, nbias_done, exp_done,
     rinv_done, probs, pT_done, p_high, p_split, pv_done, o_high, o_split, o_proj, o_added) = (s[n] for n in names)
    QW = REP * D
    pT_banks = [PP[0][:, :], PP[1][:, :], SP[1][:, 0:512], MB[:, :], SP[1][:, 512:1024]]
    P_parts = [(PH[:, t % 3, :], PL[:, t % 3, :]) for t in range(KT - 1)] + [(OH[:, :], OL[:, :])]
    q_bank = PP[1][:, :]
    qT_bank, k_bank = SP[0][:, 0:512], SP[1][:, 512:1024]
    kv_bank = SP[0][:, 512:512 + 2 * D]
    halves = lambda t: t.rearrange("p (a n) -> p a n", a=2)
    AHEAD = NPIECE + 1

    def batch_row(b):
        return resid[:, bass.ds(b, 1), :].rearrange("p a d -> p (a d)")

    with nc.Block() as block:
        @block.sync
        def _(sp):
            def load_piece(i):
                p = i + NPIECE
                sp.dma_start(Wraw[:, :], W[bass.ds(p // NPIECE, 1), :, bass.ds((p % NPIECE) * WPIECE, WPIECE)]
                             .rearrange("g p n -> p (g n)")).then_inc(w_loaded, 16)

            def load_mask(j):
                sp.dma_start(mask[:, 0:L], mask_all[:, bass.ds(j % B, 1), :].rearrange("p a n -> p (a n)"))\
                    .then_inc(mask_loaded, 16)

            def loads(i):
                ge(sp, w_split, i + 1)
                load_piece(i + AHEAD)
                ge(sp, masked, REP * i + REP)
                load_mask(i + 1)

            load_piece(NPIECE)
            load_mask(0)
            with sp.Fori(0, N_IT - 1) as i:
                loads(i)

        @block.gpsimd
        def _(pool):
            def split_x(j):
                wait_apart(pool, x_high, j + 1, v["passed"])
                v["low_part"](XL[:, :, :], XH[:, :, :], xTr[:, bass.ds(j % B, 1), :, :]).then_inc(x_split, 1)

            def split_piece(i, count):
                wait_apart(pool, w_high, count, v["passed"])
                c = v["piece_col"](i)
                v["low_part"](WL[:, bass.ds(c, WPIECE)], WH[:, bass.ds(c, WPIECE)], Wraw[:, :]).then_inc(w_split, 1)

            def step(i, last=False):
                if not last:
                    wait_apart(pool, kT_done, i + 1, v["passed"])
                    wait_apart(pool, v_split, i + 1, v["passed"])
                    gather(pool, v, i + 1)
                for h in range(REP):
                    wait_apart(pool, rinv_done, REP * i + h + 1, v["passed"])
                    pool.tensor_scalar(S[:, h, :], S[:, h, :], rinv[:, h:h + 1], 1.0, ALU.mult, ALU.mult)\
                        .then_inc(probs, 1)
                if not last:
                    split_piece(i + AHEAD, i + 2)
                    norms(i + 1)
                    split_x(i + 2)

            def norms(j):
                wait_apart(pool, q_var, j + 1, v["passed"])
                wait_apart(pool, k_var, j + 1, v["passed"])
                pool.tensor_tensor(rstd[:, :], var[:, :], neg_half[:, 0:REP + 1], ALU.pow).then_inc(rstd_done, 1)

            split_piece(NPIECE, 1)
            norms(0)
            split_x(1)
            step(0)
            with pool.Fori(1, N_IT - 1) as i:
                step(i)
            step(N_IT - 1, last=True)
            split_adapters(pool, v, 1, R3, v["adapters"][:, B * KC * R3:B * KC * R3 + DM], v["adapters3_in"],
                           a_free=(scored, REP * N_IT), b_free=(pv_done, KT * (N_IT - 1) + 2))

        @block.scalar
        def _(act):
            def q_squares(j):
                act.wait_ge(q_mults, j + 1)
                for h in range(REP):
                    last = act.activation(squares[:, h * D:(h + 1) * D], q_bank[:, h * D:(h + 1) * D], ACT.Square,
                                          accum_out=ssq[:, h:h + 1])
                last.then_inc(q_stats, 1)

            def kv(j):
                act.wait_ge(k_mults, j + 1)
                ge(act, v_split, j)
                act.activation(KV[:, KT - 1, D:2 * D], kv_bank[:, D:2 * D], ACT.Copy)
                act.activation(squares[:, QW:QW + D], kv_bank[:, 0:D], ACT.Square, accum_out=ssq[:, REP:REP + 1])\
                    .then_inc(kv_read, 1)

            def kT(j):
                act.wait_ge(kT_done, j + 1)
                ge(act, scored, REP * j)
                act.activation(KTH[:, 0:L], k_bank, ACT.Copy).then_inc(kT_high, 1)

            def qT(j):
                act.wait_ge(qT_done, j + 1)
                act.activation(QTH[:, :], qT_bank, ACT.Copy).then_inc(qT_high, 1)

            def knT(j):
                act.wait_ge(knT_done, j + 1)
                act.activation(KTH[:, L:NK], SP[0][:, 512:512 + T], ACT.Copy).then_inc(knT_high, 1)

            def v_split_high(i):
                act.wait_ge(kv_loaded, 16 * KCT * (i + 1))
                act.wait_ge(kv_read, i + 1)
                ge(act, pv_done, KT * i)
                act.activation(VH[:, :, :], KV[:, :, D:2 * D], ACT.Copy).then_inc(v_high, 1)

            def w_split_high(i, count):
                act.wait_ge(w_loaded, 16 * count)
                act.activation(WH[:, bass.ds(v["piece_col"](i), WPIECE)], Wraw[:, :], ACT.Copy).then_inc(w_high, 1)

            def exp(i, h):
                act.wait_ge(nbias_done, REP * i + h + 1)
                act.activation(S[:, h, :], S[:, h, :], ACT.Exp, bias=nbias[:, h:h + 1], scale=rstd[:, h:h + 1],
                               accum_out=rsum[:, h:h + 1]).then_inc(exp_done, 1)

            def pT(i, t):
                act.wait_ge(pT_done, KT * i + t + 1)
                if t == 3:
                    act.wait_ge(pv_done, KT * i + 1)
                act.activation(P_parts[t][0], pT_banks[t], ACT.Copy).then_inc(p_high, 1)

            def o(i):
                act.wait_ge(pv_done, KT * i + KT)
                ge(act, o_proj, i)
                act.activation(OH[:, :], MA[:, :], ACT.Copy).then_inc(o_high, 1)

            def step(i, first=False, last=False):
                v_split_high(i)
                if not first:
                    o(i - 1)
                exp(i, 0)
                exp(i, 1)
                if not last:
                    w_split_high(i + AHEAD, i + 2)
                exp(i, 2)
                exp(i, 3)
                if not last:
                    q_squares(i + 1)
                    kT(i + 1)
                for t in range(KT):
                    pT(i, t)
                    if t == 0 and not last:
                        kv(i + 1)
                if not last:
                    qT(i + 1)
                    knT(i + 1)

            kv(0)
            kT(0)
            w_split_high(NPIECE, 1)
            q_squares(0)
            qT(0)
            knT(0)
            step(0, first=True)
            with act.Fori(1, N_IT - 1) as i:
                step(i)
            step(N_IT - 1, last=True)
            o(N_IT - 1)

        @block.vector
        def _(dve):
            def x_split_high(j):
                ge(dve, kv_proj, j)
                dve.tensor_copy(XH[:, :, :], xTr[:, bass.ds(j % B, 1), :, :]
                                .rearrange("p a c t -> p (a c) t")).then_inc(x_high, 1)

            def rope_mults(j, at, n, src, table, read):
                wide = [P, n, D]
                x3 = src.rearrange("p (h d) -> p h d", h=n)
                for k, t in enumerate((rt1, rt2)):
                    last = dve.tensor_tensor(t[:, at:at + n * D].rearrange("p (h d) -> p h d", h=n), x3,
                                             tabs[:, bass.ds(j % B, 1), table + k, :].broadcast_to(wide), ALU.mult)
                last.then_inc(read, 1)

            def rope_sums(j, at, n, read, summed):
                a, b, o = (t[:, at:at + n * D].rearrange("p (h d) -> p h d", h=n) for t in (rt1, rt2, roped))
                H = D // 2
                dve.wait_ge(read, j + 1)
                dve.tensor_tensor(o[:, :, 0:H], a[:, :, 0:H], b[:, :, H:D], ALU.subtract)
                dve.tensor_tensor(o[:, :, H:D], a[:, :, H:D], b[:, :, 0:H], ALU.add).then_inc(summed, 1)

            def q_rope_mults(j):
                dve.wait_ge(q_proj, j + 1)
                ge(dve, qT_done, j)
                rope_mults(j, 0, REP, q_bank, 0, q_mults)

            def q_rope_sums(j):
                rope_sums(j, 0, REP, q_mults, q_roped)

            def q_variance(j):
                dve.wait_ge(q_stats, j + 1)
                dve.tensor_scalar(var[:, 0:REP], ssq[:, 0:REP], D * EPS, None, ALU.add).then_inc(q_var, 1)

            def k_rope(j):
                dve.wait_ge(kv_proj, j + 1)
                rope_mults(j, QW, 1, kv_bank[:, 0:D], 2, k_mults)
                rope_sums(j, QW, 1, k_mults, k_roped)

            def k_variance(j):
                dve.wait_ge(kv_read, j + 1)
                dve.tensor_scalar(var[:, REP:REP + 1], ssq[:, REP:REP + 1], 1.0 / D, EPS, ALU.mult, ALU.add)\
                    .then_inc(k_var, 1)

            def k_norm(j):
                dve.wait_ge(rstd_done, j + 1)
                dve.wait_ge(k_roped, j + 1)
                ge(dve, knT_done, j)
                dve.tensor_scalar(knew[:, :], roped[:, QW:QW + D], rstd[:, REP:REP + 1], None, ALU.mult)\
                    .then_inc(k_ready, 1)

            def kT(j):
                dve.wait_ge(kT_high, j + 1)
                dve.tensor_tensor(KTL[:, 0:L], k_bank, f32(KTH[:, 0:L]), ALU.subtract).then_inc(kT_split, 1)

            def qT(j):
                dve.wait_ge(qT_high, j + 1)
                dve.tensor_tensor(QTL[:, :], qT_bank, f32(QTH[:, :]), ALU.subtract).then_inc(qT_split, 1)

            def knT(j):
                dve.wait_ge(knT_high, j + 1)
                dve.tensor_tensor(KTL[:, L:NK], SP[0][:, 512:512 + T], f32(KTH[:, L:NK]), ALU.subtract)\
                    .then_inc(knT_split, 1)

            def mask_max(i, h):
                if h == 0:
                    dve.wait_ge(mask_loaded, 16 * (i + 1))
                    ge(dve, pT_done, KT * i)
                wait_apart(dve, scored, REP * i + h + 1, v["passed"])
                dve.tensor_tensor_reduce(out=halves(S[:, h, :]), in0=halves(SP[h % 2][:, :])[:, :, 0:NK // 2],
                                         in1=halves(mask[:, :]), scale=1.0,
                                         scalar=-3e38, op0=ALU.add, op1=ALU.max, accum_out=mx[:, h:h + 1])\
                    .then_inc(masked, 1)
                if h == 0:
                    dve.wait_ge(rstd_done, i + 1)
                dve.wait_ge(masked, REP * i + h + 1)
                dve.scalar_tensor_tensor(out=nbias[:, h:h + 1], in0=mx[:, h:h + 1], scalar=-1.0,
                                         in1=rstd[:, h:h + 1], op0=ALU.mult, op1=ALU.mult).then_inc(nbias_done, 1)

            def inverse(i, h):
                dve.wait_ge(exp_done, REP * i + h + 1)
                dve.reciprocal(rinv[:, h:h + 1], rsum[:, h:h + 1]).then_inc(rinv_done, 1)

            def pT(i, t):
                dve.wait_ge(p_high, KT * i + t + 1)
                dve.tensor_tensor(P_parts[t][1], pT_banks[t], f32(P_parts[t][0]), ALU.subtract)\
                    .then_inc(p_split, 1)

            def o(i):
                dve.wait_ge(o_high, i + 1)
                dve.tensor_tensor(OL[:, :], MA[:, :], f32(OH[:, :]), ALU.subtract).then_inc(o_split, 1)

            def o_add(i):
                dve.wait_ge(o_proj, i + 1)
                dve.tensor_tensor(batch_row(i % B), MB[:, :], batch_row(i % B), ALU.add).then_inc(o_added, 1)

            def low_v(i):
                dve.wait_ge(v_high, i + 1)
                dve.tensor_tensor(VL[:, :, :], KV[:, :, D:2 * D], f32(VH[:, :, :]), ALU.subtract).then_inc(v_split, 1)

            def step(i, first=False, last=False):
                low_v(i)
                mask_max(i, 0)
                mask_max(i, 1)
                inverse(i, 0)
                if not first:
                    o(i - 1)
                mask_max(i, 2)
                inverse(i, 1)
                mask_max(i, 3)
                inverse(i, 2)
                if not last:
                    q_rope_mults(i + 1)
                inverse(i, 3)
                if not last:
                    q_rope_sums(i + 1)
                if not first:
                    o_add(i - 1)
                if not last:
                    q_variance(i + 1)
                    kT(i + 1)
                    k_rope(i + 1)
                pT(i, 0)
                if not last:
                    k_variance(i + 1)
                pT(i, 1)
                pT(i, 2)
                if not last:
                    k_norm(i + 1)
                    x_split_high(i + 2)
                pT(i, 3)
                pT(i, 4)
                if not last:
                    qT(i + 1)
                    knT(i + 1)

            k_rope(0)
            kT(0)
            q_rope_mults(0)
            q_rope_sums(0)
            q_variance(0)
            k_variance(0)
            x_split_high(1)
            k_norm(0)
            qT(0)
            knT(0)
            step(0, first=True)
            with dve.Fori(1, N_IT - 1) as i:
                step(i)
            step(N_IT - 1, last=True)
            o(N_IT - 1)
            o_add(N_IT - 1)

        @block.tensor
        def _(pe):
            def w_half(j):
                return ((j // B) % 2) * WG

            def weights(j, at, n):
                base = w_half(j) + at
                return WH[:, bass.ds(base, n)], WL[:, bass.ds(base, n)]

            def q_project(j, chunks):
                if chunks[0] == 0:
                    pe.wait_ge(x_split, j + 1)
                    ge(pe, w_split, j)
                    ge(pe, p_split, KT * (j - 2) + 2)
                for c in chunks:
                    last = matmul3(pe, q_bank, (XH[:, c, :], XL[:, c, :]), weights(j, W_Q + c * QW, QW), c == 0,
                                   c == KC - 1)
                if chunks[-1] == KC - 1:
                    last.then_inc(q_proj, 1)

            def kv_project(j):
                ge(pe, masked, REP * j - 1)
                for c in range(KC):
                    last = matmul3(pe, kv_bank, (XH[:, c, :], XL[:, c, :]), weights(j, W_KV + c * 2 * D, 2 * D),
                                   c == 0, c == KC - 1)
                last.then_inc(kv_proj, 1)

            def k_transpose(j):
                pe.wait_ge(kv_loaded, 16 * KCT * (j + 1))
                ge(pe, masked, REP * j)
                for t in range(L // P):
                    last = pe.transpose(k_bank[:, t * P:(t + 1) * P], KV[:, t, 0:D], ident[:, :])
                last.then_inc(kT_done, 1)

            def q_transpose(j):
                pe.wait_ge(q_roped, j + 1)
                for h in range(REP):
                    last = pe.transpose(qT_bank[:, h * T:(h + 1) * T], roped[:, h * D:(h + 1) * D], ident[:, :])
                last.then_inc(qT_done, 1)

            def kn_transpose(j):
                pe.wait_ge(k_ready, j + 1)
                pe.wait_ge(kv_read, j + 1)
                pe.transpose(SP[0][:, 512:512 + T], knew[:, :], ident[:, :]).then_inc(knT_done, 1)

            def score(i, h):
                if h == 0:
                    pe.wait_ge(qT_split, i + 1)
                    pe.wait_ge(kT_split, i + 1)
                if h == 1:
                    ge(pe, p_split, KT * (i - 1) + KT)
                elif h > 1:
                    pe.wait_ge(masked, REP * i + h - 1)
                qs = QTH[:, h * T:(h + 1) * T], QTL[:, h * T:(h + 1) * T]
                for a in range(2):
                    if h == 0 and a == 1:
                        pe.wait_ge(knT_split, i + 1)
                    keys = slice(a * NK // 2, (a + 1) * NK // 2)
                    last = matmul3(pe, halves(SP[h % 2][:, :])[:, a, 0:NK // 2], qs, (KTH[:, keys], KTL[:, keys]),
                                   True, True)
                last.then_inc(scored, 1)

            def p_transpose(i, t, last_step=False):
                if t == 0:
                    pe.wait_ge(probs, REP * i + REP)
                    ge(pe, p_split, KT * i)
                if t == 1 and not last_step:
                    pe.wait_ge(q_stats, i + 2)
                if t == 3:
                    ge(pe, o_added, i)
                if t == 4 and not last_step:
                    pe.wait_ge(kT_split, i + 2)
                for h in range(REP):
                    last = pe.transpose(pT_banks[t][:, h * T:(h + 1) * T], S[:, h, t * P:(t + 1) * P], ident[:, :])
                last.then_inc(pT_done, 1)

            def pv(i, t):
                pe.wait_ge(p_split, KT * i + t + 1)
                if t == 0:
                    pe.wait_ge(v_split, i + 1)
                    ge(pe, o_split, i)
                matmul3(pe, MA[:, :], (VH[:, t, :], VL[:, t, :]), P_parts[t], t == 0,
                        t == KT - 1).then_inc(pv_done, 1)

            def o_project(i):
                pe.wait_ge(o_split, i + 1)
                ge(pe, p_split, KT * i + 4)
                for h in range(REP):
                    last = matmul3(pe, MB[:, :], (OH[:, h * T:(h + 1) * T], OL[:, h * T:(h + 1) * T]),
                                   weights(i, W_O + h * DM, DM), h == 0, h == REP - 1)
                last.then_inc(o_proj, 1)

            def step(i, first=False, last=False):
                score(i, 0)
                score(i, 1)
                if not last:
                    q_project(i + 1, (0, 1))
                score(i, 2)
                if not last:
                    q_project(i + 1, (2,))
                score(i, 3)
                if not last:
                    q_project(i + 1, (3,))
                if not first:
                    o_project(i - 1)
                if not last:
                    k_transpose(i + 1)
                    kv_project(i + 1)
                p_transpose(i, 0)
                p_transpose(i, 1, last)
                p_transpose(i, 2)
                if not last:
                    q_transpose(i + 1)
                p_transpose(i, 3)
                pv(i, 0)
                p_transpose(i, 4, last)
                pv(i, 1)
                pv(i, 2)
                if not last:
                    kn_transpose(i + 1)
                pv(i, 3)
                pv(i, 4)

            pe.wait_ge(x_split, 1)
            kv_project(0)
            k_transpose(0)
            q_project(0, range(KC))
            q_transpose(0)
            kn_transpose(0)
            step(0, first=True)
            with pe.Fori(1, N_IT - 1) as i:
                step(i)
            step(N_IT - 1, last=True)
            o_project(N_IT - 1)


def kernel(**inputs):
    import concourse.bacc as bacc
    from concourse.bass_utils import run_bass_kernel_spmd

    a = {k: np.asarray(x) for k, x in inputs.items()}

    def chunks(w):
        return w.T.reshape(-1, P, w.shape[0]).transpose(1, 0, 2)

    f = np.float32
    W = np.zeros((HK + 2, P, WG), f)
    W[0, :, W_BASE0:W_BASE0 + KC * DM] = chunks(a["L0_cond_W"]).reshape(P, -1)
    ar = np.concatenate([a["L0_cond_A"].reshape(E * R0, DM), a["L0_cond_Wr"]], 0)
    W[0, :, W_AR:W_AR + KC * AR] = chunks(ar).reshape(P, -1)
    W[0, :, W_BASE1:] = chunks(a["L1_cond_W"]).reshape(P, -1)
    W[HK + 1, :, W_BASE3:] = chunks(a["L3_cond_W"]).reshape(P, -1)
    for g in range(HK):
        rows = slice(g * REP * D, (g + 1) * REP * D)
        kv = np.concatenate([a["L2_cond_Wk"][g * D:(g + 1) * D], a["L2_cond_Wv"][g * D:(g + 1) * D]], 0)
        W[g + 1, :, W_Q:W_KV] = chunks(a["L2_cond_Wq"][rows]).reshape(P, -1)
        W[g + 1, :, W_KV:W_O] = chunks(kv).reshape(P, -1)
        W[g + 1, :, W_O:] = a["L2_cond_Wo"][:, rows].T.reshape(REP, D, DM).transpose(1, 0, 2).reshape(P, -1)
    half_pow = (10000.0 ** (np.arange(0, D, 2) / D)).astype(f)
    arrays = {
        "x": np.ascontiguousarray(a["x"]),
        "xT": np.ascontiguousarray(a["x"].reshape(B, T, KC, P).transpose(3, 0, 2, 1)),
        "W": W,
        "a1": np.ascontiguousarray(a["L1_cond_lora_A"].reshape(-1, KC, P, R1).transpose(0, 2, 1, 3))
        .reshape(-1, P, KC * R1),
        "b1": np.ascontiguousarray(a["L1_cond_lora_B_w"].T),
        "a3": np.ascontiguousarray(a["L3_cond_lora_As"].reshape(-1, KC, P, R3).transpose(0, 2, 1, 3))
        .reshape(-1, KC * R3),
        "b3": a["L3_cond_lora_Bs"].reshape(-1, DM),
        "bcat0": np.ascontiguousarray(a["L0_cond_B"].transpose(0, 2, 1).reshape(E * R0, DM)),
        "bias3": np.ascontiguousarray(a["L3_cond_b"]),
        "kv_cache": np.concatenate([a["L2_cond_k_cache"], a["L2_cond_v_cache"]], -1).transpose(2, 0, 1, 3)
        .reshape(HK * PAGES * PSIZE, 2 * D),
        "table": np.ascontiguousarray(a["itok_Bx16_0_63"].reshape(B, KCT, P // PSIZE).transpose(2, 0, 1))
        .reshape(P // PSIZE, B * KCT),
        "q_w": np.ascontiguousarray(a["L2_cond_q_norm_w"]),
        "k_w": np.ascontiguousarray(a["L2_cond_k_norm_w"]),
        "inv_freq": f(1) / half_pow,
        "ids": np.concatenate([a["itok_B_0_2"], a["itok_B_0_23"],
                               a["itok_B_207_1644"], a["itok_B_0_7"]]),
    }
    nc = bacc.Bacc("TRN2", target_bir_lowering=False, num_devices=1)
    args = {k: nc.dram_tensor(f"in_{k}", x.shape, mybir.dt.from_np(x.dtype), kind="ExternalInput").ap()
            for k, x in arrays.items()}
    out = nc.dram_tensor("out_0", (B, T, DM), FP32, kind="ExternalOutput").ap()
    build(nc, out=out, **args)
    r = run_bass_kernel_spmd(nc, [{f"in_{k}": x for k, x in arrays.items()}], core_ids=[0])
    return r.results[0]["out_0"]
```
